# Optimizing a Trainium2 kernel written in Bass

```python
import numpy as np
import jax
import jax.numpy as jnp

def _softmax(x, axis=-1):
    return jax.nn.softmax(x, axis=axis)

def _gelu(x):
    return jax.nn.gelu(x, approximate=True)

def _silu(x):
    return jax.nn.silu(x)

def _sigmoid(x):
    return jax.nn.sigmoid(x)

def _layernorm(x, axis=-1, eps=1e-05):
    m = jnp.mean(x, axis=axis, keepdims=True)
    v = jnp.var(x, axis=axis, keepdims=True)
    return (x - m) / jnp.sqrt(v + eps)

def _scatter_add(tgt, idx, src, axis=0):
    return tgt.at[idx].add(src)

def _segment_sum(src, seg, n):
    return jax.ops.segment_sum(src, seg, n)
kernel_name = 'mk_gnn_preln_d1_gnn_r64_b63972'

def setup_inputs(seed: int=0):
    np.random.seed(seed)
    _w = jnp.asarray

    def _rec_inputs():
        import jax
        import jax.numpy as jnp
        _gk = jax.random.key(seed)
        x = -0.000202 + 1 * jax.random.normal(jax.random.fold_in(_gk, 1), (100000, 64), jnp.float32)
        src = jax.random.randint(jax.random.fold_in(_gk, 2), (50000,), 0, 100000, jnp.int32)
        dst = jax.random.randint(jax.random.fold_in(_gk, 3), (50000,), 0, 100000, jnp.int32)
        _o = jnp.argsort(dst, stable=True)
        src = src[_o]
        dst = dst[_o]
        edge_attr_64 = -5.16925e-05 + 1.00005 * jax.random.normal(jax.random.fold_in(_gk, 12), (50000, 64), jnp.float32)
        return (x, src, dst, edge_attr_64)
    x, src, dst, edge_attr_64 = _rec_inputs()

    def _L0_gnn_setup():
        import jax, jax.numpy as jnp
        import numpy as np
        N_NODES = 100000
        N_EDGES = 25000
        N_GRAPHS = 512
        D = 64
        BN_EPS = 1e-05

        def _batchnorm(h, gamma, beta):
            mean = jnp.mean(h, axis=0)
            var = jnp.var(h, axis=0)
            return (h - mean) * jax.lax.rsqrt(var + BN_EPS) * gamma + beta
        key = jax.random.key(seed)
        ks = jax.random.split(key, 16)
        x = jax.random.normal(ks[0], (N_NODES, D), dtype=jnp.float32)
        edge_index = jax.random.randint(ks[1], (2, N_EDGES), 0, N_NODES, dtype=jnp.int64)
        edge_attr = jax.random.normal(ks[2], (N_EDGES, D), dtype=jnp.float32)
        global_attr = jax.random.normal(ks[3], (N_GRAPHS, D), dtype=jnp.float32)
        batch = jnp.sort(jax.random.randint(ks[4], (N_NODES,), 0, N_GRAPHS, dtype=jnp.int64))
        W1 = jax.random.normal(ks[5], (3 * D, D), dtype=jnp.float32) / np.sqrt(3 * D)
        b1 = jnp.zeros((D,), dtype=jnp.float32)
        W2 = jax.random.normal(ks[6], (D, D), dtype=jnp.float32) / np.sqrt(D)
        b2 = jnp.zeros((D,), dtype=jnp.float32)
        W3 = jax.random.normal(ks[7], (D, D), dtype=jnp.float32) / np.sqrt(D)
        b3 = jnp.zeros((D,), dtype=jnp.float32)
        g1 = jnp.ones((D,), dtype=jnp.float32)
        bt1 = jnp.zeros((D,), dtype=jnp.float32)
        g2 = jnp.ones((D,), dtype=jnp.float32)
        bt2 = jnp.zeros((D,), dtype=jnp.float32)
        g3 = jnp.ones((D,), dtype=jnp.float32)
        bt3 = jnp.zeros((D,), dtype=jnp.float32)
        return dict(x=x, edge_index=edge_index, edge_attr=edge_attr, global_attr=global_attr, batch=batch, W1=W1, b1=b1, W2=W2, b2=b2, W3=W3, b3=b3, g1=g1, bt1=bt1, g2=g2, bt2=bt2, g3=g3, bt3=bt3)
    _L0_gnn_all = _L0_gnn_setup()
    _L0_gnn_in = {k: v for k, v in _L0_gnn_all.items() if k in ('global_attr', 'W1', 'b1', 'W2', 'b2', 'W3', 'b3', 'g1', 'bt1', 'g2', 'bt2', 'g3', 'bt3')}
    del _L0_gnn_all
    return {'x': x, 'src': src, 'dst': dst, 'edge_attr_64': edge_attr_64, 'L0_gnn_global_attr': _L0_gnn_in['global_attr'], 'L0_gnn_W1': _L0_gnn_in['W1'], 'L0_gnn_b1': _L0_gnn_in['b1'], 'L0_gnn_W2': _L0_gnn_in['W2'], 'L0_gnn_b2': _L0_gnn_in['b2'], 'L0_gnn_W3': _L0_gnn_in['W3'], 'L0_gnn_b3': _L0_gnn_in['b3'], 'L0_gnn_g1': _L0_gnn_in['g1'], 'L0_gnn_bt1': _L0_gnn_in['bt1'], 'L0_gnn_g2': _L0_gnn_in['g2'], 'L0_gnn_bt2': _L0_gnn_in['bt2'], 'L0_gnn_g3': _L0_gnn_in['g3'], 'L0_gnn_bt3': _L0_gnn_in['bt3']}

def reference(x, src, dst, edge_attr_64, L0_gnn_global_attr, L0_gnn_W1, L0_gnn_b1, L0_gnn_W2, L0_gnn_b2, L0_gnn_W3, L0_gnn_b3, L0_gnn_g1, L0_gnn_bt1, L0_gnn_g2, L0_gnn_bt2, L0_gnn_g3, L0_gnn_bt3):
    import jax
    import jax.numpy as jnp

    def _L0_gnn_ref(x, edge_index, edge_attr, global_attr, batch, W1, b1, W2, b2, W3, b3, g1, bt1, g2, bt2, g3, bt3):
        import jax, jax.numpy as jnp
        import numpy as np
        N_NODES = 100000
        N_EDGES = 25000
        N_GRAPHS = 512
        D = 64
        BN_EPS = 1e-05

        def _batchnorm(h, gamma, beta):
            mean = jnp.mean(h, axis=0)
            var = jnp.var(h, axis=0)
            return (h - mean) * jax.lax.rsqrt(var + BN_EPS) * gamma + beta
        src = edge_index[0]
        sums = jax.ops.segment_sum(edge_attr, src, num_segments=N_NODES)
        counts = jax.ops.segment_sum(jnp.ones((edge_attr.shape[0],), edge_attr.dtype), src, num_segments=N_NODES)
        v_e = sums / jnp.maximum(counts, 1.0)[:, None]
        comb = jnp.concatenate([x, v_e, global_attr[batch]], axis=1)
        out = _batchnorm(jax.nn.relu(comb @ W1 + b1), g1, bt1)
        out = _batchnorm(jax.nn.relu(out @ W2 + b2), g2, bt2)
        out = _batchnorm(jax.nn.relu(out @ W3 + b3), g3, bt3)
        return out
    edge_index = jnp.stack([src, dst])
    batch0 = jnp.zeros((100000,), jnp.int32)
    h = jnp.maximum(_layernorm(x, axis=-1), 0.0)
    x = x + _L0_gnn_ref(h, edge_index, edge_attr_64, L0_gnn_global_attr, batch0, L0_gnn_W1, L0_gnn_b1, L0_gnn_W2, L0_gnn_b2, L0_gnn_W3, L0_gnn_b3, L0_gnn_g1, L0_gnn_bt1, L0_gnn_g2, L0_gnn_bt2, L0_gnn_g3, L0_gnn_bt3)
    return x

_drawn_inputs = setup_inputs


def setup_inputs(seed=0):
    import zlib

    import numpy as np

    out = dict(_drawn_inputs(seed))
    spreads = {'L0_gnn_b1': (0.0, 0.1),
     'L0_gnn_b2': (0.0, 0.1),
     'L0_gnn_b3': (0.0, 0.1),
     'L0_gnn_g1': (1.0, 0.2),
     'L0_gnn_bt1': (0.0, 0.1),
     'L0_gnn_g2': (1.0, 0.2),
     'L0_gnn_bt2': (0.0, 0.1),
     'L0_gnn_g3': (1.0, 0.2),
     'L0_gnn_bt3': (0.0, 0.1)}
    factors = {}
    for name, (base, spread) in spreads.items():
        noise = np.random.default_rng([zlib.crc32(name.encode()), seed]).standard_normal(out[name].shape)
        drawn = base * np.exp(spread * noise) if base else spread * noise
        out[name] = jnp.asarray(drawn.astype(out[name].dtype))
    for name, factor in factors.items():
        out[name] = (out[name] * factor).astype(out[name].dtype)
    return out
```

```python
from contextlib import ExitStack

import concourse.bass as bass
from concourse import mybir

ALU = mybir.AluOpType
ACT = mybir.ActivationFunctionType
BF16 = mybir.dt.bfloat16
F32 = mybir.dt.float32
I32 = mybir.dt.int32
U32 = mybir.dt.uint32

P = 128
D = 64
G = 8
H = G // 2
ROW = D + 1
LOW = ROW + 1
NG = 8
CH = P * NG
COLS = CH // 2
EPS = 1e-5
TARGETS_AT = 4
AHEAD = 16
IN_Z = 70
GRAIN = 22
GRAINS = 36
CLEARS = 2


def build_kernel(nc, x, src, edge_attr, global_attr, W1, b1, W2, b2, W3, b3, g1, bt1, g2, bt2, g3, bt3, out):
    N = x.shape[0]
    NE = edge_attr.shape[0]
    FULL = N // CH
    TP = 112
    TG = (N - FULL * CH) // TP
    NC = FULL + 1
    TCOLS = TP * TG // 2
    HALF = N // 2
    PAIRS = FULL // 2
    assert TP * TG == N - FULL * CH and TG % 2 == 0 and FULL * COLS + TCOLS == HALF and FULL % 6 == 1
    EG = G * P
    EFULL = NE // EG
    EP = (NE - EFULL * EG) // G
    NGR = EFULL + 1
    STEPS = 2 * NGR
    assert EP * G == NE - EFULL * EG and 0 < EP <= P and EFULL % 2 == 0
    TROWS = P * GRAIN * GRAINS
    assert TROWS >= N + EG
    SCR = IN_Z * COLS
    LOOPS = EFULL // 2
    PARK = (IN_Z - AHEAD + 2) // 4
    XEND = (NC - AHEAD) // 4
    assert 4 * PARK + AHEAD - 2 == IN_Z and NC - AHEAD - 4 * XEND == 2
    FIRST_CLEARS = (GRAINS - (AHEAD - 4) * CLEARS) // 4
    assert 4 * FIRST_CLEARS + (AHEAD - 4) * CLEARS == GRAINS
    LATE = FULL - IN_Z
    assert LATE % 3 == 0

    table = nc.dram_tensor("edge_sums", (TROWS, ROW), F32, kind="Internal").ap()
    table_by_partition = table.rearrange("(p n r) c -> p n (r c)", p=P, r=GRAIN)
    parked = nc.dram_tensor("parked", (LATE * P, COLS), F32, kind="Internal").ap()
    parked_tail = nc.dram_tensor("parked_tail", (P, TCOLS), F32, kind="Internal").ap()

    with ExitStack() as ctx:
        def sb(name, shape, dt):
            return ctx.enter_context(nc.sbuf_tensor(name, shape, dt))

        def sem(name):
            return ctx.enter_context(nc.semaphore(name))

        ps = ctx.enter_context(nc.psum_tensor("ps", [P, 8, 512], F32))

        Z = sb("Z", [P, HALF], F32)
        work = sb("work", [P, 5, NG * ROW], F32)
        ident = sb("ident", [P, P], F32)
        Wa = sb("Wa", [P, P], F32)
        Wb = sb("Wb", [P, P], F32)
        vec = sb("vec", [P, 28], F32)
        small = sb("small", [P, 13, NG], F32)

        at = [SCR]

        def scratch(cols):
            a = at[0]
            at[0] += cols
            assert at[0] <= HALF, at[0]
            return Z[:, a:a + cols]

        def scratch16(*shape):
            n = 1
            for k in shape:
                n *= k
            t = scratch(n // 2).bitcast(BF16)
            return t.rearrange("p (j e) -> p j e", j=shape[0]) if len(shape) == 2 else t

        ids = [scratch(EG).bitcast(I32) for _ in range(2)]
        edges = [scratch(G * D) for _ in range(2)]
        high_mid = [scratch16(G, P) for _ in range(2)]
        low_one = [scratch16(G, LOW) for _ in range(2)]
        sel = [scratch16(H, H * P), scratch16(G, H * P)]
        sel_upto = [scratch16(H, P) for _ in range(2)]
        upto = scratch16(1, P)
        pick = scratch16(LOW)
        rest = [scratch(H * D) for _ in range(2)]
        sums_hm = scratch(H * P)
        sums_lo = scratch(H * P)
        rows = [[scratch(H * LOW) for _ in range(2)] for _ in range(2)]
        W1b_hm = scratch(LOW)
        W1b_lo = scratch(LOW)
        srci = [scratch(G).bitcast(I32) for _ in range(2)]
        srcf = [scratch(G) for _ in range(2)]
        seen0 = [scratch(G) for _ in range(2)]
        seen1 = [scratch(G) for _ in range(2)]
        gap = scratch(G)
        seen = scratch(G)
        later = scratch(G)
        masked = scratch(G)
        target = [scratch(G).bitcast(U32) for _ in range(2)]
        spare = scratch(G)
        spare_i = scratch(G).bitcast(I32)
        stats_x = [scratch(NG * 6) for _ in range(2)]
        h_tile = [scratch(COLS) for _ in range(2)]
        park_tile = [scratch(COLS) for _ in range(2)]
        W1c2 = scratch(P)
        g0 = scratch(1)
        zero = Z[:, SCR - GRAIN * ROW:SCR]

        (DIFF, M2, DIFF2, NSUM, NVAR, NSTD, NRSTD, NSHIFT) = (0, 1, 2, 3, 5, 7, 9, 11)

        def sm(row, n, q):
            return small[0:n, row, 0:q]

        def wk(i):
            return work[:, i, :]

        def nodes_of(dram, c, tail=False):
            if tail:
                return dram[FULL * CH:N, :].rearrange("(p g) c -> p (g c)", p=TP)
            return dram[bass.ds(c * CH, CH), :].rearrange("(p g) c -> p (g c)", p=P)

        def zc(c, tail=False, n=1):
            return Z[:, FULL * COLS:HALF] if tail else Z[:, bass.ds(c * COLS, n * COLS)]

        (B1, B2, B3, G1, T1, G2, T2, G3, T3, BIAS1, BIAS2, BIAS3, EPSC, MEAN, VAR, MEANC, DEV, DEV2, Q, VARC, STD,
         RSTD, SCALE, MS, SHIFT, SCALE3, SHIFT3) = range(27)

        def v(i, n=1):
            return vec[:, i:i + n]

        weights_in = sem("weights_in")
        edges_in = [sem(f"edges_in{i}") for i in range(2)]
        x_in = [sem(f"x_in{i}") for i in range(4)]
        table_zeroed = sem("table_zeroed")
        rows_added = sem("rows_added")
        parked_out = [sem(f"parked_out{i}") for i in range(2)]
        parked_in = sem("parked_in")
        sums_in = [sem(f"sums_in{i}") for i in range(3)]
        W3_in = sem("W3_in")
        x_again = [sem(f"x_again{i}") for i in range(3)]
        out_stored = sem("out_stored")
        consts = sem("consts")
        fconst = sem("fconst")
        shared_ready = sem("shared_ready")
        bias1_ready = sem("bias1_ready")
        high_ready = sem("high_ready")
        rest_ready = sem("rest_ready")
        mid_ready = sem("mid_ready")
        low_ready = sem("low_ready")
        srcf_ready = sem("srcf_ready")
        sel_ready = sem("sel_ready")
        upto_ready = sem("upto_ready")
        target_steps = sem("target_steps")
        target_ready = sem("target_ready")
        summed = sem("summed")
        sums_copied = sem("sums_copied")
        y_ready = sem("y_ready")
        rows_ready = sem("rows_ready")
        ln_steps = sem("ln_steps")
        var_ready = sem("var_ready")
        std_ready = sem("std_ready")
        rstd_ready = sem("rstd_ready")
        norm_ready = sem("norm_ready")
        h_ready = sem("h_ready")
        hT_ready = sem("hT_ready")
        hT_kept = sem("hT_kept")
        floor_ready = sem("floor_ready")
        inv_ready = sem("inv_ready")
        means_ready = sem("means_ready")
        meansT_ready = sem("meansT_ready")
        meansT_kept = sem("meansT_kept")
        a1_ready = sem("a1_ready")
        added = sem("added")
        z1_ready = sem("z1_ready")
        z1_seen = sem("z1_seen")
        a_ready = [sem(f"a{i}_ready") for i in (2, 3)]
        z_ready = [sem(f"z{i}_ready") for i in (2, 3)]
        z_seen = [sem(f"z{i}_seen") for i in (2, 3)]
        fold_pe = sem("fold_pe")
        fold_dve = sem("fold_dve")
        fold_act = sem("fold_act")
        affine_ready = sem("affine_ready")
        zT_ready = sem("zT_ready")
        out_ready = sem("out_ready")

        FOLD = [3 + 12 * layer for layer in range(3)]
        MEAN_READY = [f + 1 for f in FOLD]
        Q_READY = [f + 5 for f in FOLD]
        VAR_READY = [f + 6 for f in FOLD]
        SHIFT_READY = [f + 10 for f in FOLD]
        BIAS_READY = [f + 11 for f in FOLD]
        WEIGHTS_READY = [f + 12 for f in FOLD]

        SELS = H + G
        ADDED = 16 * G

        weight_loads = []
        for h in range(2):
            q = slice(h * D, (h + 1) * D)
            weight_loads += [(Wa[q, q], W1[0:D, :]), (Wb[q, q], W2[:, :]), (W1b_hm[q, 0:D], W1[D:2 * D, :]),
                             (W1c2[0:D, q], W1[2 * D:3 * D, :])]
            for i, a in ((B1, b1), (B2, b2), (B3, b3), (G1, g1), (T1, bt1), (G2, g2), (T2, bt2), (G3, g3), (T3, bt3)):
                weight_loads.append((vec[q, i:i + 1], a.rearrange("(p a) -> p a", a=1)))
        weight_loads += [(W1b_lo[0:D, 0:D], W1[D:2 * D, :]), (g0[0:D, :], global_attr[0:1, :].rearrange("a p -> p a"))]

        def tiles_of(h):
            return [(j, max(0, j - H * h)) for j in range(H * (h + 1))]

        block = ctx.enter_context(nc.Block())

        @block.sync
        def _(sp):
            def load_edges(g, b, free, tail=False):
                if free:
                    sp.wait_ge(sel_ready, SELS * (g - 1))
                    nc.sync.nop(nofuse=True)
                    sp.wait_ge(srcf_ready, g - 1)
                    nc.sync.nop(nofuse=True)
                    sp.wait_ge(rest_ready, 2 * (g - 1))
                    nc.sync.nop(nofuse=True)
                n = EP if tail else P
                e = slice(EFULL * EG, NE) if tail else bass.ds(g * EG, EG)
                sp.dma_start(srci[b][0:n, :], src[e].rearrange("(p j) -> p j", j=G)).then_inc(edges_in[b], 16)
                sp.dma_start(ids[b][0:n, 0:n * G], src[e].rearrange("(a e) -> a e", a=1).broadcast_to([n, n * G])
                             ).then_inc(edges_in[b], 16)
                sp.dma_start(edges[b][0:n, :], edge_attr[e, :].rearrange("(p j) c -> p (j c)", j=G)
                             ).then_inc(edges_in[b], 16)

            def load_x(c, slot, free, tail=False):
                if free:
                    sp.wait_ge(h_ready, c - 3)
                    nc.sync.nop(nofuse=True)
                n, k = (TP, TG) if tail else (P, NG)
                sp.dma_start(wk(slot)[0:n, 0:k * D], nodes_of(x, c, tail)).then_inc(x_in[slot], 16)

            def park(c, b, tail=False):
                sp.wait_ge(hT_kept, c + 1)
                nc.sync.nop(nofuse=True)
                if tail:
                    sp.dma_start(parked_tail, park_tile[b][:, 0:TCOLS]).then_inc(parked_out[b], 16)
                else:
                    sp.dma_start(parked[bass.ds((c - IN_Z) * P, P), :], park_tile[b]).then_inc(parked_out[b], 16)

            for c in range(4):
                load_x(c, c, False)
            load_edges(0, 0, False)
            load_edges(1, 1, False)
            for c in range(4, 6):
                load_x(c, c % 4, True)
            with sp.Fori(1, AHEAD // 4) as k:
                for i in range(4):
                    load_x(4 * k + i + 2, (i + 2) % 4, True)

            def step(k, i, parks=False, loads=True):
                if loads:
                    load_x(4 * k + i + AHEAD + 2, (i + 2) % 4, True)
                if i % 2 == 0:
                    load_edges(2 * k + i // 2 + 1, (i // 2 + 1) % 2, True)
                if parks:
                    park(4 * k + i + AHEAD - 2, i % 2)

            for i in range(4):
                if i == 0:
                    load_x(AHEAD + 2, 2, True)
                else:
                    step(0, i)
            with sp.Fori(1, PARK) as k:
                for i in range(4):
                    step(k, i)
            with sp.Fori(PARK, XEND - 1) as k:
                for i in range(4):
                    step(k, i, parks=True)
            for i in range(2):
                step(XEND - 1, i, parks=True)
            load_x(FULL - 1, 0, True)
            load_edges(2 * XEND, 0, True)
            park(FULL - 5, 0)
            load_x(FULL, 1, True, tail=True)
            park(FULL - 4, 1)
            for i in range(3):
                step(XEND, i, parks=True, loads=False)
            park(FULL, 1, tail=True)
            with sp.Fori(XEND + 1, LOOPS - 1) as k:
                for i in range(4):
                    step(k, i, loads=False)
            step(LOOPS - 1, 0, loads=False)
            load_edges(EFULL, 0, True, tail=True)

            def load_sums(c, r, free, tail=False):
                if free:
                    sp.wait_ge(means_ready, c - 2)
                n, k = (TP, TG) if tail else (P, NG)
                sp.dma_start(wk(r)[0:n, 0:k * ROW], nodes_of(table, c, tail)).then_inc(sums_in[r], 16)

            sp.wait_ge(h_ready, NC)
            sp.wait_ge(rows_added, 16 * G * NGR)
            for r in range(3):
                load_sums(r, r, False)
            sp.wait_ge(hT_kept, NC)
            for b in range(2):
                sp.wait_ge(parked_out[b], 16 * ((NC - IN_Z) // 2 + (b == 1) * ((NC - IN_Z) % 2)))
            sp.dma_start(Z[:, FULL * COLS:HALF], parked_tail).then_inc(parked_in, 16)
            for c in range(3, 6):
                load_sums(c, c % 3, True)
            with sp.Fori(1, 1 + LATE // 3) as k:
                for i in range(6):
                    load_sums(6 * k + i, i % 3, True)
                sp.dma_start(zc(IN_Z - 3 + 3 * k, n=3).rearrange("p (n c) -> p n c", c=COLS),
                             parked[bass.ds((3 * k - 3) * P, 3 * P), :].rearrange("(n p) c -> p n c", p=P)
                             ).then_inc(parked_in, 16)
            with sp.Fori(1 + LATE // 3, FULL // 6) as k:
                for i in range(6):
                    load_sums(6 * k + i, i % 3, True)
            load_sums(FULL - 1, 0, True)
            load_sums(FULL, 1, True, tail=True)

            sp.wait_ge(z1_seen, NC)
            for h in range(2):
                sp.dma_start(Wa[h * D:(h + 1) * D, h * D:(h + 1) * D], W3[:, :]).then_inc(W3_in, 16)

            def reload_x(c, s, free, tail=False):
                if free:
                    sp.wait_ge(out_ready, c - 2)
                n, k = (TP, TG) if tail else (P, NG)
                sp.dma_start(wk(s)[0:n, 0:k * D], nodes_of(x, c, tail)).then_inc(x_again[s], 16)

            def store(c, tail=False):
                sp.wait_ge(out_ready, c + 1)
                n = TP if tail else P
                k = TG if tail else NG
                sp.dma_start(nodes_of(out, c, tail), wk(FULL % 3)[0:n, 0:k * D] if tail else zc(c)
                             ).then_inc(out_stored, 16)

            for c in range(3):
                reload_x(c, c, False)
            with sp.Fori(0, (FULL - 4) // 3) as k:
                for s in range(3):
                    store(3 * k + s)
                    reload_x(3 * k + s + 3, s, True)
            for c in range(FULL - 4, NC):
                store(c, tail=(c == FULL))
                if c + 3 < NC:
                    reload_x(c + 3, c % 3, True, tail=(c + 3 == FULL))
            sp.wait_ge(out_stored, 16 * NC)

        @block.gpsimd
        def _(pool):
            nc.gpsimd.memset(zero, 0.0).then_inc(consts, 1)
            nc.gpsimd.memset(Wa[:, :], 0.0).then_inc(consts, 1)
            nc.gpsimd.memset(Wb[:, :], 0.0).then_inc(consts, 1)
            nc.gpsimd.memset(W1b_hm, 0.0).then_inc(consts, 1)
            nc.gpsimd.memset(W1b_lo, 0.0).then_inc(consts, 1)
            nc.gpsimd.memset(v(EPSC), EPS).then_inc(consts, 1)
            nc.gpsimd.memset(ident[:, :], 0.0).then_inc(consts, 1)
            nc.gpsimd.memset(upto, 1.0).then_inc(consts, 1)
            nc.gpsimd.memset(pick[:, 0:ROW], 0.0).then_inc(fconst, 1)
            nc.gpsimd.memset(pick[:, ROW:LOW], 1.0).then_inc(fconst, 1)
            for b in range(2):
                nc.gpsimd.memset(low_one[b][:, :, D:ROW], 1.0).then_inc(fconst, 1)
                nc.gpsimd.memset(low_one[b][:, :, ROW:LOW], 0.0).then_inc(fconst, 1)
                nc.gpsimd.memset(seen0[b], 0.0).then_inc(fconst, 1)
            nc.gpsimd.iota(spare_i, pattern=[[P, G]], base=N, channel_multiplier=1).then_inc(fconst, 1)
            pool.wait_ge(consts, 8)
            nc.gpsimd.affine_select(out=ident[:, :], in_=ident[:, :], compare_op=ALU.not_equal, fill=1.0, base=0,
                                    pattern=[[-1, P]], channel_multiplier=1).then_inc(fconst, 1)
            nc.gpsimd.affine_select(out=upto[:, 0, :], in_=upto[:, 0, :], compare_op=ALU.is_ge, fill=0.0, base=0,
                                    pattern=[[1, P]], channel_multiplier=-1).then_inc(fconst, 1)
            pool.wait_ge(fconst, 11)
            nc.gpsimd.tensor_copy(W1b_lo[D:P, D:LOW], ident[D:P, D:LOW]).then_inc(fconst, 1)
            for dst, a in weight_loads:
                pool.dma_start(dst, a).then_inc(weights_in, 16)

            pool.wait_ge(table_zeroed, 16 * GRAINS)

            def scatter(g, b, tail=False):
                n = EP if tail else P
                pool.wait_ge(rows_ready, 2 * g + 2)
                pool.wait_ge(target_ready, g + 1)
                pool.wait_ge(rows_added, ADDED * g)
                nc.gpsimd.nop(nofuse=True)
                for j in range(G):
                    i = j % H
                    nc.gpsimd.indirect_dma_start(
                        out=table, out_offset=bass.IndirectOffsetOnAxis(ap=target[b][0:n, j:j + 1], axis=0),
                        in_=rows[b][j // H][0:n, i * LOW:i * LOW + ROW], in_offset=None,
                        compute_op=ALU.add).then_inc(rows_added, 16)

            scatter(0, 0)
            scatter(1, 1)
            with pool.Fori(1, LOOPS) as k:
                scatter(2 * k, 0)
                scatter(2 * k + 1, 1)
            scatter(EFULL, 0, tail=True)

            def means(c, r, b, free, tail=False):
                n, k = (TP, TG) if tail else (P, NG)
                pool.wait_ge(inv_ready, c + 1)
                if free:
                    pool.wait_ge(meansT_ready, c - 1)
                nc.gpsimd.tensor_tensor(
                    wk(3 + b)[0:n, 0:k * D].rearrange("p (g c) -> p g c", c=D),
                    wk(r)[0:n, 0:k * ROW].rearrange("p (g c) -> p g c", c=ROW)[:, :, 0:D],
                    sm(3 + r, n, k).rearrange("p (g c) -> p g c", c=1).broadcast_to([n, k, D]),
                    ALU.mult).then_inc(means_ready, 1)

            for i in range(6):
                means(i, i % 3, i % 2, i > 1)
            with pool.Fori(1, FULL // 6) as k:
                for i in range(6):
                    means(6 * k + i, i % 3, i % 2, True)
            means(FULL - 1, 0, 0, True)
            means(FULL, 1, 1, True, tail=True)

        @block.vector
        def _(dve):
            def same_node(s, g, b, h, k, first, between, tail=False):
                n = EP if tail else P
                if h == 0:
                    dve.wait_ge(edges_in[b], 48 * (k + 1))
                    if not first:
                        dve.wait_ge(target_ready, g - 1)
                    nc.vector.tensor_copy(srcf[b][0:n, :], srci[b][0:n, :]).then_inc(srcf_ready, 1)
                if not first:
                    dve.wait_ge(summed, s - 1)
                dve.wait_ge(srcf_ready, g + 1)
                cols = ids[b][0:n, 0:n * G].rearrange("q (p i) -> q i p", i=G)
                count = seen0[b] if h == 0 else seen1[b]
                for j, first_col in tiles_of(h):
                    nc.vector.tensor_scalar(
                        sel[h][0:n, j, first_col * n:H * n].rearrange("q (i p) -> q i p", p=n),
                        cols[:, H * h + first_col:H * (h + 1), :], srcf[b][0:n, j:j + 1], 0.0, ALU.is_equal, ALU.add,
                        accum_out=count[0:n, j:j + 1]).then_inc(sel_ready, 1)
                    for part in between[j]:
                        part()

            def own_tile(s, g, h, tail=False):
                n = EP if tail else P
                dve.wait_ge(sel_ready, SELS * g + (H if h == 0 else SELS))
                blocks = sel[h].rearrange("p j e -> p (j e)")[0:n, H * h * H * P:]
                a = diag_view(blocks, n)
                nc.vector.tensor_tensor(sel_upto[h][0:n, :, 0:n], a, upto[0:n, :, 0:n].broadcast_to([n, H, n]),
                                        ALU.mult).then_inc(upto_ready, 1)

            def diag_view(blocks, n):
                return bass.AP(blocks.tensor, blocks.offset, [blocks.ap[0], [H * P + n, H], [1, n]])

            def edge_rest(s, b, h, free, tail=False):
                n = EP if tail else P
                q = slice(h * H, (h + 1) * H)
                dve.wait_ge(high_ready, s + 1)
                if free:
                    dve.wait_ge(low_ready, s - 1)
                nc.vector.tensor_tensor(rest[h][0:n, :].rearrange("p (j c) -> p j c", j=H),
                                        edges[b][0:n, :].rearrange("p (j c) -> p j c", j=G)[:, q, :],
                                        high_mid[b][0:n, q, 0:D], ALU.subtract).then_inc(rest_ready, 1)

            def edge_low(s, b, h, tail=False):
                n = EP if tail else P
                q = slice(h * H, (h + 1) * H)
                dve.wait_ge(mid_ready, s + 1)
                nc.vector.tensor_tensor(low_one[b][0:n, q, 0:D], rest[h][0:n, :].rearrange("p (j c) -> p j c", j=H),
                                        high_mid[b][0:n, q, D:P], ALU.subtract).then_inc(low_ready, 1)

            TS = 5

            def targets(g, b, free, tail=False):
                n = EP if tail else P

                def gap_and_seen():
                    nc.vector.tensor_tensor(gap[0:n, :], spare[0:n, :], srcf[b][0:n, :],
                                            ALU.subtract).then_inc(target_steps, 1)
                    nc.vector.tensor_tensor(seen[0:n, :], seen0[b][0:n, :], seen1[b][0:n, :],
                                            ALU.add).then_inc(target_steps, 1)

                def later_ones():
                    dve.wait_ge(rows_ready, 2 * g + 2)
                    dve.wait_ge(target_steps, TS * g + 2)
                    for h in range(2):
                        q = slice(h * H, (h + 1) * H)
                        nc.vector.tensor_tensor(later[0:n, q], seen[0:n, q], rows[b][h][0:n, :].rearrange(
                            "p (j c) -> p j c", c=LOW)[:, :, ROW], ALU.subtract).then_inc(target_steps, 1)

                def mask():
                    dve.wait_ge(target_steps, TS * g + 4)
                    nc.vector.scalar_tensor_tensor(out=masked[0:n, :], in0=later[0:n, :], scalar=1.0, in1=gap[0:n, :],
                                                   op0=ALU.min, op1=ALU.mult).then_inc(target_steps, 1)

                def place():
                    dve.wait_ge(target_steps, TS * g + 5)
                    if free:
                        dve.wait_ge(rows_added, ADDED * (g - 1))
                    nc.vector.tensor_tensor(target[b][0:n, :], masked[0:n, :], srcf[b][0:n, :],
                                            ALU.add).then_inc(target_ready, 1)

                return [gap_and_seen, later_ones, mask, place]

            LN = NG + 4

            def ln_stats(c, b, slot, use, tail=False):
                n, q = (TP, TG) if tail else (P, NG)
                dve.wait_ge(x_in[slot], 16 * (use + 1))
                for g in range(q):
                    nc.vector.bn_stats(stats_x[b][0:n, g * 6:(g + 1) * 6], wk(slot)[0:n, g * D:(g + 1) * D]
                                       ).then_inc(ln_steps, 1 + (NG - q) * (g == 0))

            def ln_sums(c, b, tail=False):
                n, q = (TP, TG) if tail else (P, NG)
                st = stats_x[b][0:n, 0:q * 6].rearrange("p (g s) -> p g s", s=6)
                dve.wait_ge(ln_steps, LN * c + NG)
                nc.vector.tensor_tensor(sm(DIFF, n, q), st[:, :, 1], st[:, :, 4], ALU.subtract).then_inc(ln_steps, 1)
                nc.vector.tensor_tensor(sm(NSUM + b, n, q), st[:, :, 1], st[:, :, 4], ALU.add).then_inc(ln_steps, 1)
                nc.vector.tensor_tensor(sm(M2, n, q), st[:, :, 2], st[:, :, 5], ALU.add).then_inc(ln_steps, 1)

            def ln_square(c, b, tail=False):
                n, q = (TP, TG) if tail else (P, NG)
                dve.wait_ge(ln_steps, LN * c + NG + 3)
                nc.vector.tensor_tensor(sm(DIFF2, n, q), sm(DIFF, n, q), sm(DIFF, n, q), ALU.mult).then_inc(ln_steps, 1)

            def ln_var(c, b, tail=False):
                n, q = (TP, TG) if tail else (P, NG)
                dve.wait_ge(ln_steps, LN * c + NG + 4)
                nc.vector.scalar_tensor_tensor(out=sm(NVAR + b, n, q), in0=sm(DIFF2, n, q), scalar=D / 4.0,
                                               in1=sm(M2, n, q), op0=ALU.mult, op1=ALU.add).then_inc(var_ready, 1)

            def ln_rstd(c, b, free, tail=False):
                n, q = (TP, TG) if tail else (P, NG)
                dve.wait_ge(std_ready, c + 1)
                if free:
                    dve.wait_ge(h_ready, c - 1)
                nc.vector.reciprocal(sm(NRSTD + b, n, q), sm(NSTD + b, n, q)).then_inc(rstd_ready, 1)

            def ln_shift(c, b, tail=False):
                n, q = (TP, TG) if tail else (P, NG)
                dve.wait_ge(rstd_ready, c + 1)
                nc.vector.scalar_tensor_tensor(out=sm(NSHIFT + b, n, q), in0=sm(NSUM + b, n, q), scalar=-0.5,
                                               in1=sm(NRSTD + b, n, q), op0=ALU.mult, op1=ALU.mult).then_inc(norm_ready, 1)

            dve.wait_ge(fconst, 12)
            nc.vector.tensor_copy(spare, spare_i).then_inc(fconst, 1)
            dve.wait_ge(fconst, 13)

            def x_only(k, i, first=False):
                c = 4 * k + i
                if not first:
                    ln_rstd(c - 1, (i + 1) % 2, i > 2 or not isinstance(k, int))
                ln_stats(c, i % 2, i, k)
                if not first:
                    ln_shift(c - 1, (i + 1) % 2)
                ln_sums(c, i % 2)
                ln_square(c, i % 2)
                ln_var(c, i % 2)

            x_only(0, 0, True)
            for i in range(1, 4):
                x_only(0, i)
            with dve.Fori(1, AHEAD // 4) as k:
                for i in range(4):
                    x_only(k, i)
            dve.wait_ge(shared_ready, 1)
            nc.vector.tensor_tensor(v(BIAS1), v(B1), ps[:, 5, 500:501], ALU.add).then_inc(bias1_ready, 1)
            edge_rest(0, 0, 0, False)

            def step(k, i, x=True, x_before=True, first=False, tail=False, next_tail=False, last=False, x_tail=False,
                     before_tail=False):
                s, g, h, b = 4 * k + i, 2 * k + i // 2, i % 2, i // 2
                c, cb, u = s + AHEAD, i % 2, k + AHEAD // 4
                if x:
                    ln_stats(c, cb, i, u, x_tail)
                between = [[] for _ in range(G)]
                if x:
                    for j, part in enumerate((ln_sums, ln_square, ln_var)):
                        between[j].append(lambda part=part: part(c, cb, x_tail))
                if h == 1 and not (first and i < 4):
                    for j, part in enumerate(targets(g - 1, 1 - b, not first)):
                        between[j + TARGETS_AT].append(part)
                if x_before:
                    between[2].append(lambda: ln_rstd(c - 1, 1 - cb, True, before_tail))
                    between[3].append(lambda: ln_shift(c - 1, 1 - cb, before_tail))
                if first and i == 2:
                    between[3] += targets(0, 0, False)
                same_node(s, g, b, h, k, first and i < 2, between, tail)
                edge_low(s, b, h, tail)
                own_tile(s, g, h, tail)
                if not last:
                    edge_rest(s + 1, ((i + 1) // 2) % 2, 1 - h, not (first and i == 0), next_tail)

            for i in range(4):
                step(0, i, first=True)
            with dve.Fori(1, XEND) as k:
                for i in range(4):
                    step(k, i)
            step(XEND, 0)
            step(XEND, 1, x_tail=True)
            step(XEND, 2, x=False, before_tail=True)
            step(XEND, 3, x=False, x_before=False)
            with dve.Fori(XEND + 1, LOOPS - 1) as k:
                for i in range(4):
                    step(k, i, x=False, x_before=False)
            for i in range(4):
                step(LOOPS - 1, i, x=False, x_before=False, next_tail=(i == 3))
            step(LOOPS, 0, x=False, x_before=False, tail=True, next_tail=True)
            step(LOOPS, 1, x=False, x_before=False, tail=True, last=True)
            for part in targets(EFULL, 0, True, tail=True):
                part()

            dve.wait_ge(hT_ready, NC)
            dve.wait_ge(h_ready, NC)

            def invert(c, r, use, tail=False):
                n, q = (TP, TG) if tail else (P, NG)
                dve.wait_ge(sums_in[r], 16 * (use + 1))
                cnt = wk(r)[0:n, 0:q * ROW].rearrange("p (g c) -> p g c", c=ROW)[:, :, D]
                nc.vector.tensor_scalar(sm(r, n, q), cnt, 1.0, None, ALU.max).then_inc(floor_ready, 1)

            def inverse(c, r, free, tail=False):
                n, q = (TP, TG) if tail else (P, NG)
                dve.wait_ge(floor_ready, c + 1)
                if free:
                    dve.wait_ge(means_ready, c - 2)
                nc.vector.reciprocal(sm(3 + r, n, q), sm(r, n, q)).then_inc(inv_ready, 1)

            def add(c, r, tail=False):
                w = TCOLS if tail else COLS
                dve.wait_ge(a1_ready, c + 1)
                dve.wait_ge(meansT_kept, c + 1)
                nc.vector.tensor_tensor(zc(c, tail), ps[:, r, 0:w], zc(c, tail), ALU.add).then_inc(added, 1)

            def see(k, b, ready, seen_sem, tail=False):
                c = 2 * k + b
                dve.wait_ge(ready, c + 1)
                nc.vector.bn_stats(ps[:, 6 + b, bass.ds(k * 6, 6)], zc(c, tail)).then_inc(seen_sem, 1)

            def layer1(k, i, first=False, tail=False):
                c = 6 * k + i
                invert(c, i % 3, 2 * k + i // 3, tail)
                inverse(c, i % 3, not (first and i < 3), tail)
                if not (first and i < 2):
                    add(c - 2, (i - 2) % 3)
                if not (first and i < 5):
                    see(3 * k + (i - 5) // 2, (i - 5) % 2, z1_ready, z1_seen)

            for i in range(6):
                layer1(0, i, first=True)
            with dve.Fori(1, FULL // 6) as k:
                for i in range(6):
                    layer1(k, i)
            layer1(FULL // 6, 0)
            layer1(FULL // 6, 1, tail=True)
            add(FULL - 1, (FULL - 1) % 3)
            see(PAIRS - 2, 1, z1_ready, z1_seen)
            add(FULL, FULL % 3, tail=True)
            see(PAIRS - 1, 0, z1_ready, z1_seen)
            see(PAIRS - 1, 1, z1_ready, z1_seen)
            see(PAIRS, 0, z1_ready, z1_seen)
            see(PAIRS, 1, z1_ready, z1_seen, tail=True)

            done = [0]

            def chain(ins):
                done[0] += 1
                ins.then_inc(fold_dve, 1)
                dve.wait_ge(fold_dve, done[0])

            def fold(layer, seen_sem, gi, ti, scale, shift):
                dve.wait_ge(seen_sem, NC)
                chain(nc.vector.bn_aggr(v(MEAN, 2), ps[:, 6:8, 0:3 * NC]))
                dve.wait_ge(fold_pe, 3 * layer + 1)
                chain(nc.vector.tensor_copy(v(MEANC), ps[:, 5, 0:1]))
                chain(nc.vector.tensor_tensor(v(DEV), v(MEAN), v(MEANC), ALU.subtract))
                chain(nc.vector.tensor_tensor(v(DEV2), v(DEV), v(DEV), ALU.mult))
                chain(nc.vector.tensor_tensor(v(Q), v(DEV2), v(VAR), ALU.add))
                dve.wait_ge(fold_pe, 3 * layer + 2)
                chain(nc.vector.tensor_copy(v(VARC), ps[:, 5, 1:2]))
                dve.wait_ge(fold_act, layer + 1)
                chain(nc.vector.reciprocal(v(RSTD), v(STD)))
                chain(nc.vector.tensor_tensor(v(scale), v(gi), v(RSTD), ALU.mult))
                chain(nc.vector.tensor_tensor(v(MS), v(MEANC), v(scale), ALU.mult))
                chain(nc.vector.tensor_tensor(v(shift), v(ti), v(MS), ALU.subtract))

            def average():
                chain(nc.vector.tensor_tensor(wk(4)[:, P:P + D], ident[:, 0:D], ident[:, D:P], ALU.add))
                for h in range(2):
                    chain(nc.vector.tensor_scalar(wk(4)[:, h * D:(h + 1) * D], wk(4)[:, P:P + D], 0.5, None, ALU.mult))

            average()
            fold(0, z1_seen, G1, T1, SCALE, SHIFT)
            dve.wait_ge(fold_pe, 3)
            chain(nc.vector.tensor_tensor(v(BIAS2), ps[:, 5, 2:3], v(B2), ALU.add))
            chain(nc.vector.tensor_scalar(Wb[:, :], Wb[:, :], v(SCALE), None, ALU.mult))

            for layer in (1, 2):
                ready, seen_sem = z_ready[layer - 1], z_seen[layer - 1]
                with dve.Fori(0, PAIRS) as k:
                    for b in range(2):
                        see(k, b, ready, seen_sem)
                see(PAIRS, 0, ready, seen_sem)
                see(PAIRS, 1, ready, seen_sem, tail=True)
                if layer == 1:
                    fold(1, seen_sem, G2, T2, SCALE, SHIFT)
                    dve.wait_ge(fold_pe, 6)
                    chain(nc.vector.tensor_tensor(v(BIAS3), ps[:, 5, 2:3], v(B3), ALU.add))
                    chain(nc.vector.tensor_scalar(Wa[:, :], Wa[:, :], v(SCALE), None, ALU.mult))
                else:
                    fold(2, seen_sem, G3, T3, SCALE3, SHIFT3)

            def finish(c, b, s, use, tail=False):
                n, w = (TP, TG * D) if tail else (P, COLS)
                dve.wait_ge(x_again[s], 16 * (use + 1))
                dve.wait_ge(zT_ready, c + 1)
                o = wk(s)[0:n, 0:w] if tail else zc(c)
                nc.vector.tensor_tensor(o, ps[0:n, b, 0:w], wk(s)[0:n, 0:w], ALU.add).then_inc(out_ready, 1)

            with dve.Fori(0, FULL // 6) as k:
                for i in range(6):
                    finish(6 * k + i, i % 2, i % 3, 2 * k + i // 3)
            for c in range(FULL // 6 * 6, NC):
                finish(c, c % 2, c % 3, c // 3, tail=(c == FULL))

        @block.scalar
        def _(act):
            act.wait_ge(consts, 8)

            def high(s, b, h, k, free, tail=False):
                n = EP if tail else P
                q = slice(h * H, (h + 1) * H)
                act.wait_ge(edges_in[b], 48 * (k + 1))
                if free:
                    act.wait_ge(summed, s - 2 - h)
                nc.scalar.copy(high_mid[b][0:n, q, 0:D],
                               edges[b][0:n, :].rearrange("p (j c) -> p j c", j=G)[:, q, :]).then_inc(high_ready, 1)

            def mid(s, b, h, tail=False):
                n = EP if tail else P
                act.wait_ge(rest_ready, s + 1)
                nc.scalar.copy(high_mid[b][0:n, h * H:(h + 1) * H, D:P],
                               rest[h][0:n, :].rearrange("p (j c) -> p j c", j=H)).then_inc(mid_ready, 1)

            def sums(s, h, tail=False):
                w = (EP if tail else P) * H
                act.wait_ge(summed, s + 1)
                act.wait_ge(y_ready, s)
                nc.scalar.copy(sums_hm[:, 0:w], ps[:, h, 0:w]).then_inc(sums_copied, 1)
                nc.scalar.copy(sums_lo[0:LOW, 0:w], ps[0:LOW, 2 + h, 0:w]).then_inc(sums_copied, 1)

            def row(s, g, b, h, free, tail=False):
                n = EP if tail else P
                act.wait_ge(y_ready, s + 1)
                if free:
                    act.wait_ge(rows_added, ADDED * (g - 1))
                nc.scalar.copy(rows[b][h][0:n, :], ps[0:n, 4 + h, 0:H * LOW]).then_inc(rows_ready, 1)

            def std(c, b, tail=False):
                n, q = (TP, TG) if tail else (P, NG)
                act.wait_ge(var_ready, c + 1)
                nc.scalar.activation(sm(NSTD + b, n, q), sm(NVAR + b, n, q), ACT.Sqrt, bias=v(EPSC)[0:n, :],
                                     scale=1.0 / D).then_inc(std_ready, 1)

            def normed(c, b, slot, free, tail=False):
                n, q = (TP, TG) if tail else (P, NG)
                act.wait_ge(norm_ready, c + 1)
                if free:
                    act.wait_ge(hT_ready, c - 1)
                for g in range(q):
                    ins = nc.scalar.activation(h_tile[b][0:n, g * D:(g + 1) * D], wk(slot)[0:n, g * D:(g + 1) * D],
                                               ACT.Relu, bias=small[0:n, NSHIFT + b, g:g + 1],
                                               scale=small[0:n, NRSTD + b, g:g + 1])
                ins.then_inc(h_ready, 1)

            def keep(c, b, dst, wait=None, tail=False):
                w = TCOLS if tail else COLS
                act.wait_ge(hT_ready, c + 1)
                if wait is not None:
                    act.wait_ge(parked_out[b], wait)
                nc.scalar.copy(dst[:, 0:w], ps[:, 6 + b, 0:w]).then_inc(hT_kept, 1)

            def x_only(k, i, first=False):
                c = 4 * k + i
                std(c, i % 2)
                if not (first and i < 2):
                    keep(c - 2, i % 2, zc(c - 2))
                if not (first and i < 1):
                    normed(c - 1, (i + 1) % 2, (i + 3) % 4, not (first and i < 3))

            def clear(first, n):
                for j in range(n):
                    act.dma_start(table_by_partition[:, bass.ds(first + j, 1), :].rearrange("p n c -> p (n c)"),
                                  zero).then_inc(table_zeroed, 16)

            for i in range(4):
                clear(i * FIRST_CLEARS, FIRST_CLEARS)
                x_only(0, i, first=True)
            with act.Fori(1, AHEAD // 4) as k:
                for i in range(4):
                    clear(4 * FIRST_CLEARS - 4 * CLEARS + (4 * k + i) * CLEARS, CLEARS)
                    x_only(k, i)
            high(0, 0, 0, 0, False)

            def step(k, i, x=True, x_before=True, where="Z", first=False, tail=False, next_tail=False, last=False,
                     x_tail=False, before_tail=False, kept_tail=False):
                s, g, h, b = 4 * k + i, 2 * k + i // 2, i % 2, i // 2
                c, cb = s + AHEAD, i % 2
                mid(s, b, h, tail)
                if not last:
                    high(s + 1, ((i + 1) % 4) // 2, 1 - h, k + (i == 3), not (first and i < 3), next_tail)
                if not (first and i == 0):
                    sums(s - 1, 1 - h, tail and h == 1)
                if where == "Z":
                    keep(c - 2, cb, zc(c - 2))
                elif where is not None:
                    keep(c - 2, cb, park_tile[cb], 16 * (2 * (k - PARK) + i // 2) if where == "DRAM" else None,
                         kept_tail)
                if x_before:
                    normed(c - 1, 1 - cb, (i + 3) % 4, True, before_tail)
                if not (first and i == 0):
                    pb = ((i + 3) % 4) // 2
                    row(s - 1, 2 * k + (i - 1) // 2, pb, 1 - h, not first, tail and h == 1)
                if x:
                    std(c, cb, x_tail)

            for i in range(4):
                step(0, i, first=True)
            with act.Fori(1, PARK) as k:
                for i in range(4):
                    step(k, i)
            for i in range(4):
                step(PARK, i, where="park" if i < 2 else "DRAM")
            with act.Fori(PARK + 1, XEND) as k:
                for i in range(4):
                    step(k, i, where="DRAM")
            step(XEND, 0, where="DRAM")
            step(XEND, 1, where="DRAM", x_tail=True)
            step(XEND, 2, x=False, where="DRAM", before_tail=True)
            step(XEND, 3, x=False, x_before=False, where="DRAM", kept_tail=True)
            with act.Fori(XEND + 1, LOOPS - 1) as k:
                for i in range(4):
                    step(k, i, x=False, x_before=False, where=None)
            for i in range(4):
                step(LOOPS - 1, i, x=False, x_before=False, where=None, next_tail=(i == 3))
            step(LOOPS, 0, x=False, x_before=False, where=None, tail=True, next_tail=True)
            step(LOOPS, 1, x=False, x_before=False, where=None, tail=True, last=True)
            sums(STEPS - 1, 1, tail=True)
            row(STEPS - 1, EFULL, 0, 1, True, tail=True)

            def keep_means(c, b, tail=False):
                w = TCOLS if tail else COLS
                act.wait_ge(meansT_ready, c + 1)
                act.wait_ge(a1_ready, c + 1)
                nc.scalar.copy(zc(c, tail), ps[:, 3 + b, 0:w]).then_inc(meansT_kept, 1)

            def relu1(c, tail=False):
                act.wait_ge(added, c + 1)
                nc.scalar.activation(zc(c, tail), zc(c, tail), ACT.Relu, bias=v(BIAS1)).then_inc(z1_ready, 1)

            act.wait_ge(bias1_ready, 1)
            for c in range(4):
                keep_means(c, c % 2)
            relu1(0)
            with act.Fori(2, PAIRS) as k:
                keep_means(2 * k, 0)
                relu1(2 * k - 3)
                keep_means(2 * k + 1, 1)
                relu1(2 * k - 2)
            keep_means(FULL - 1, 0)
            relu1(FULL - 4)
            keep_means(FULL, 1, tail=True)
            relu1(FULL - 3)
            relu1(FULL - 2)
            relu1(FULL - 1)
            relu1(FULL, tail=True)

            for layer in range(3):
                act.wait_ge(fold_dve, VAR_READY[layer])
                nc.scalar.activation(v(STD), v(VARC), ACT.Sqrt, bias=v(EPSC)).then_inc(fold_act, 1)
                if layer == 2:
                    break
                act.wait_ge(fold_dve, BIAS_READY[layer])
                bias = v(BIAS2 if layer == 0 else BIAS3)

                def relu(c, b, n=2, tail=False):
                    if tail:
                        s, d = ps[:, 2, 0:TCOLS], zc(0, True)
                    elif n == 1:
                        s, d = ps[:, 0, :], zc(c)
                    else:
                        s, d = ps[:, 2 * b:2 * b + 2, :], zc(c, n=2).rearrange("p (b n) -> p b n", b=2)
                    act.wait_ge(a_ready[layer], c + n)
                    nc.scalar.activation(d, s, ACT.Relu, bias=bias).then_inc(z_ready[layer], n)

                with act.Fori(0, PAIRS // 2) as k:
                    relu(4 * k, 0)
                    relu(4 * k + 2, 1)
                relu(FULL - 1, 0, n=1)
                relu(FULL, 1, n=1, tail=True)

            act.wait_ge(fold_dve, SHIFT_READY[2])

            def affine(c, b, free, tail=False):
                w = TCOLS if tail else COLS
                if free:
                    act.wait_ge(zT_ready, c - 1)
                nc.scalar.activation(wk(3 + b)[:, 0:w], zc(c, tail), ACT.Identity, bias=v(SHIFT3),
                                     scale=v(SCALE3)).then_inc(affine_ready, 1)

            affine(0, 0, False)
            affine(1, 1, False)
            with act.Fori(1, PAIRS) as k:
                affine(2 * k, 0, True)
                affine(2 * k + 1, 1, True)
            affine(FULL - 1, 0, True)
            affine(FULL, 1, True, tail=True)

        @block.tensor
        def _(pe):
            pe.wait_ge(fconst, 13)

            def sums(s, g, b, h, free, tail=False):
                n = EP if tail else P
                w = n * H
                if free:
                    pe.wait_ge(sums_copied, 2 * (s - 1))
                pe.wait_ge(mid_ready, s + 1)
                last = H * (h + 1) - 1
                for j, first_col in tiles_of(h):
                    q = slice(first_col * n, w)
                    pe.wait_ge(sel_ready, SELS * g + H * h + j + 1)
                    nc.tensor.matmul(ps[:, h, q], high_mid[b][0:n, j, :], sel[h][0:n, j, q],
                                     start=(j == 0), stop=(j == last))
                pe.wait_ge(low_ready, s + 1)
                lo = ps[0:LOW, 2 + h, :]
                for j, first_col in tiles_of(h):
                    q = slice(first_col * n, w)
                    nc.tensor.matmul(lo[:, q], low_one[b][0:n, j, :], sel[h][0:n, j, q], start=(j == 0), stop=False)
                pe.wait_ge(upto_ready, s + 1)
                nc.tensor.matmul(lo[:, 0:w], pick[0:n, :], sel_upto[h][0:n, :, 0:n],
                                 start=False, stop=True).then_inc(summed, 1)

            def products(s, h, free, tail=False):
                n = EP if tail else P
                pe.wait_ge(sums_copied, 2 * (s + 1))
                if free:
                    pe.wait_ge(rows_ready, s - 1)
                for i in range(H):
                    q = slice(i * n, (i + 1) * n)
                    o = ps[0:n, 4 + h, i * LOW:(i + 1) * LOW]
                    nc.tensor.matmul(o, sums_hm[:, q], W1b_hm, start=True, stop=False)
                    ins = nc.tensor.matmul(o, sums_lo[0:LOW, q], W1b_lo[0:LOW, :], start=False, stop=True)
                ins.then_inc(y_ready, 1)

            def turn(c, b, free, tail=False):
                n, q = (TP, TG) if tail else (P, NG)
                pe.wait_ge(h_ready, c + 1)
                if free:
                    pe.wait_ge(hT_kept, c - 1)
                for j in range(q // 2):
                    ins = nc.tensor.transpose(ps[:, 6 + b, j * n:(j + 1) * n], h_tile[b][0:n, j * P:(j + 1) * P],
                                              ident[0:n, 0:n])
                ins.then_inc(hT_ready, 1)

            for c in range(2):
                turn(c, c % 2, False)
            with pe.Fori(1, AHEAD // 4) as k:
                for i in range(4):
                    turn(4 * k + i - 2, i % 2, True)
            pe.wait_ge(weights_in, 16 * len(weight_loads))
            nc.tensor.matmul(ps[:, 5, 500:501], W1c2[0:D, :], g0[0:D, :], start=True, stop=True).then_inc(shared_ready, 1)

            def step(k, i, x_before=True, first=False, tail=False, kept_tail=False):
                s, g, h, b = 4 * k + i, 2 * k + i // 2, i % 2, i // 2
                if x_before:
                    turn(s + AHEAD - 2, h, True, kept_tail)
                if not (first and i == 0):
                    products(s - 1, 1 - h, not (first and i < 3), tail and h == 1)
                sums(s, g, b, h, not (first and i < 2), tail)

            for i in range(4):
                step(0, i, first=True)
            with pe.Fori(1, XEND) as k:
                for i in range(4):
                    step(k, i)
            for i in range(4):
                step(XEND, i, kept_tail=(i == 3))
            with pe.Fori(XEND + 1, LOOPS) as k:
                for i in range(4):
                    step(k, i, x_before=False)
            for i in range(2):
                step(LOOPS, i, x_before=False, tail=True)
            products(STEPS - 1, 1, True, tail=True)

            pe.wait_ge(hT_kept, NC)
            pe.wait_ge(rows_ready, STEPS)

            def product1(c, r, free, tail=False):
                w = TCOLS if tail else COLS
                if free:
                    pe.wait_ge(added, c - 2)
                nc.tensor.matmul(ps[:, r, 0:w], Wa[:, :], zc(c, tail), start=True, stop=True).then_inc(a1_ready, 1)

            def turn_means(c, b, free, tail=False):
                n, q = (TP, TG) if tail else (P, NG)
                pe.wait_ge(means_ready, c + 1)
                if free:
                    pe.wait_ge(meansT_kept, c - 1)
                for j in range(q // 2):
                    ins = nc.tensor.transpose(ps[:, 3 + b, j * n:(j + 1) * n], wk(3 + b)[0:n, j * P:(j + 1) * P],
                                              ident[0:n, 0:n])
                ins.then_inc(meansT_ready, 1)

            for c in range(6):
                if c > 0:
                    turn_means(c - 1, (c - 1) % 2, c > 2)
                product1(c, c % 3, c > 2)
            SPLIT = IN_Z // 6
            for a, z in ((1, SPLIT), (SPLIT, FULL // 6)):
                if a == SPLIT:
                    pe.wait_ge(parked_in, 16 * (1 + LATE // 3))
                with pe.Fori(a, z) as k:
                    for i in range(6):
                        turn_means(6 * k + i - 1, (i - 1) % 2, True)
                        product1(6 * k + i, i % 3, True)
            turn_means(FULL - 2, 1, True)
            product1(FULL - 1, 0, True)
            turn_means(FULL - 1, 0, True)
            product1(FULL, 1, True, tail=True)
            turn_means(FULL, 1, True, tail=True)

            def fold(layer):
                pe.wait_ge(fold_dve, MEAN_READY[layer])
                nc.tensor.matmul(ps[:, 5, 0:1], wk(4)[:, 0:P], v(MEAN), start=True, stop=True).then_inc(fold_pe, 1)
                pe.wait_ge(fold_dve, Q_READY[layer])
                nc.tensor.matmul(ps[:, 5, 1:2], wk(4)[:, 0:P], v(Q), start=True, stop=True).then_inc(fold_pe, 1)
                if layer == 2:
                    return
                pe.wait_ge(fold_dve, SHIFT_READY[layer])
                W = Wb if layer == 0 else Wa
                if layer == 1:
                    pe.wait_ge(W3_in, 32)
                nc.tensor.matmul(ps[:, 5, 2:3], W[:, :], v(SHIFT), start=True, stop=True).then_inc(fold_pe, 1)

            fold(0)
            for layer in (1, 2):
                W = Wb if layer == 1 else Wa
                pe.wait_ge(fold_dve, WEIGHTS_READY[layer - 1])
                ready, done = a_ready[layer - 1], z_ready[layer - 1]

                def product(c, bank, wait, tail=False):
                    w = TCOLS if tail else COLS
                    if wait is not None:
                        pe.wait_ge(done, wait)
                    nc.tensor.matmul(ps[:, bank, 0:w], W[:, :], zc(c, tail), start=True, stop=True).then_inc(ready, 1)

                for c in range(4):
                    product(c, c, None)
                with pe.Fori(1, PAIRS // 2) as k:
                    for i in range(4):
                        product(4 * k + i, i, 4 * k - 2 + i if i % 2 == 0 else None)
                product(FULL - 1, 0, FULL - 3)
                product(FULL, 2, FULL - 1, tail=True)
                fold(layer)

            def turn_back(c, b, free, tail=False):
                n, q = (TP, TG) if tail else (P, NG)
                pe.wait_ge(affine_ready, c + 1)
                if free:
                    pe.wait_ge(out_ready, c - 1)
                for j in range(q // 2):
                    ins = nc.tensor.transpose(ps[0:n, b, j * P:(j + 1) * P], wk(3 + b)[:, j * n:(j + 1) * n],
                                              ident[:, :])
                ins.then_inc(zT_ready, 1)

            turn_back(0, 0, False)
            turn_back(1, 1, False)
            with pe.Fori(1, PAIRS) as k:
                turn_back(2 * k, 0, True)
                turn_back(2 * k + 1, 1, True)
            turn_back(FULL - 1, 0, True)
            turn_back(FULL, 1, True, tail=True)


_INS = ["x", "src", "edge_attr_64", "L0_gnn_global_attr", "L0_gnn_W1", "L0_gnn_b1", "L0_gnn_W2", "L0_gnn_b2", "L0_gnn_W3",
        "L0_gnn_b3", "L0_gnn_g1", "L0_gnn_bt1", "L0_gnn_g2", "L0_gnn_bt2", "L0_gnn_g3", "L0_gnn_bt3"]


def kernel(**inputs):
    import numpy as _np
    import concourse.bacc as _bacc
    from concourse import mybir as _mybir
    from concourse.bass_utils import run_bass_kernel_spmd as _run

    nc = _bacc.Bacc("TRN2", target_bir_lowering=False, num_devices=1)
    arrays, args = {}, []
    for name in _INS:
        a = _np.ascontiguousarray(inputs[name])
        arrays[f"in_{name}_dram"] = a
        args.append(nc.dram_tensor(f"in_{name}_dram", a.shape, _mybir.dt.from_np(a.dtype), kind="ExternalInput").ap())
    shape = inputs["x"].shape
    out = nc.dram_tensor("out_0_dram", shape, _mybir.dt.float32, kind="ExternalOutput").ap()
    build_kernel(nc, *args, out)
    r = _run(nc, [arrays], core_ids=[0])
    return r.results[0]["out_0_dram"]
```

```python
from contextlib import ExitStack

import concourse.bass as bass
from concourse import mybir

ALU = mybir.AluOpType
ACT = mybir.ActivationFunctionType
BF16 = mybir.dt.bfloat16
F32 = mybir.dt.float32
I32 = mybir.dt.int32
U32 = mybir.dt.uint32

P = 128
D = 64
G = 8
H = G // 2
ROW = D + 1
LOW = ROW + 1
NG = 8
CH = P * NG
COLS = CH // 2
EPS = 1e-5
PRODUCTS_AT = 3
LOW_AT = 3
TARGETS_AT = 4
AHEAD = 16
IN_Z = 70
GRAIN = 22
GRAINS = 36
FIRST_CLEARS = 3
CLEARS = 1


def build_kernel(nc, x, src, edge_attr, global_attr, W1, b1, W2, b2, W3, b3, g1, bt1, g2, bt2, g3, bt3, out):
    N = x.shape[0]
    NE = edge_attr.shape[0]
    FULL = N // CH
    TP = 112
    TG = (N - FULL * CH) // TP
    NC = FULL + 1
    TCOLS = TP * TG // 2
    HALF = N // 2
    PAIRS = FULL // 2
    assert TP * TG == N - FULL * CH and TG % 2 == 0 and FULL * COLS + TCOLS == HALF and FULL % 6 == 1
    EG = G * P
    EFULL = NE // EG
    EP = (NE - EFULL * EG) // G
    NGR = EFULL + 1
    STEPS = 2 * NGR
    assert EP * G == NE - EFULL * EG and 0 < EP <= P and EFULL % 2 == 0
    TROWS = P * GRAIN * GRAINS
    assert TROWS >= N + EG
    SCR = IN_Z * COLS
    LOOPS = EFULL // 2
    PARK = (IN_Z - AHEAD + 2) // 4
    XEND = (NC - AHEAD) // 4
    assert 4 * PARK + AHEAD - 2 == IN_Z and NC - AHEAD - 4 * XEND == 2
    LAST_CLEARS = GRAINS // 4 - FIRST_CLEARS - (AHEAD // 4 - 1) * CLEARS
    assert LAST_CLEARS >= 0 and GRAINS % 4 == 0 and AHEAD % 4 == 0
    assert AHEAD <= IN_Z // 2 and (IN_Z // 2 + AHEAD) * COLS <= IN_Z * COLS - GRAIN * ROW
    LATE = FULL - IN_Z
    assert FULL % 4 == 1 and LATE // 2 < IN_Z // 4

    table = nc.dram_tensor("edge_sums", (TROWS, ROW), F32, kind="Internal").ap()
    table_by_partition = table.rearrange("(p n r) c -> p n (r c)", p=P, r=GRAIN)
    parked = nc.dram_tensor("parked", (LATE * P, COLS), F32, kind="Internal").ap()
    parked_tail = nc.dram_tensor("parked_tail", (P, TCOLS), F32, kind="Internal").ap()

    with ExitStack() as ctx:
        def sb(name, shape, dt):
            return ctx.enter_context(nc.sbuf_tensor(name, shape, dt))

        def sem(name):
            return ctx.enter_context(nc.semaphore(name))

        ps = ctx.enter_context(nc.psum_tensor("ps", [P, 8, 512], F32))

        Z = sb("Z", [P, HALF], F32)
        work = sb("work", [P, 5, NG * ROW], F32)
        ident = sb("ident", [P, P], F32)
        Wa = sb("Wa", [P, P], F32)
        Wb = sb("Wb", [P, P], F32)
        vec = sb("vec", [P, 28], F32)
        small = sb("small", [P, 14, NG], F32)

        at = [SCR]

        def scratch(cols):
            a = at[0]
            at[0] += cols
            assert at[0] <= HALF, at[0]
            return Z[:, a:a + cols]

        def scratch16(*shape):
            n = 1
            for k in shape:
                n *= k
            t = scratch(n // 2).bitcast(BF16)
            return t.rearrange("p (j e) -> p j e", j=shape[0]) if len(shape) == 2 else t

        ids = [scratch(EG).bitcast(I32) for _ in range(2)]
        edges = [scratch(G * D) for _ in range(2)]
        high_mid = [scratch16(G, P) for _ in range(2)]
        low_one = [scratch16(G, LOW) for _ in range(2)]
        sel = [scratch16(H, H * P), scratch16(G, H * P)]
        sel_upto = [scratch16(H, P) for _ in range(2)]
        upto = scratch16(1, P)
        pick = scratch16(LOW)
        rest = [scratch(H * D) for _ in range(2)]
        sums_hm = scratch(H * P)
        sums_lo = scratch(H * P)
        rows = [scratch(G * LOW) for _ in range(2)]
        W1b_hm = scratch(LOW)
        W1b_lo = scratch(LOW)
        srci = [scratch(G).bitcast(I32) for _ in range(2)]
        srcf = [scratch(G) for _ in range(2)]
        seen0 = [scratch(G) for _ in range(2)]
        seen1 = [scratch(G) for _ in range(2)]
        gap = scratch(G)
        seen = scratch(G)
        later = scratch(G)
        masked = scratch(G)
        target = [scratch(G).bitcast(U32) for _ in range(2)]
        spare = scratch(G)
        spare_i = scratch(G).bitcast(I32)
        stats_x = [scratch(NG * 6) for _ in range(2)]
        h_tile = [scratch(COLS) for _ in range(2)]
        park_tile = [scratch(COLS) for _ in range(2)]
        W1c2 = scratch(P)
        g0 = scratch(1)
        zero = Z[:, SCR - GRAIN * ROW:SCR]

        (DIFF, DIFF2, NSUM, NVAR, NSTD, NRSTD, NSHIFT) = (0, 1, 2, 6, 8, 10, 12)

        def sm(row, n, q):
            return small[0:n, row, 0:q]

        def wk(i):
            return work[:, i, :]

        def nodes_of(dram, c, tail=False):
            if tail:
                return dram[FULL * CH:N, :].rearrange("(p g) c -> p (g c)", p=TP)
            return dram[bass.ds(c * CH, CH), :].rearrange("(p g) c -> p (g c)", p=P)

        def zc(c, tail=False, n=1):
            return Z[:, FULL * COLS:HALF] if tail else Z[:, bass.ds(c * COLS, n * COLS)]

        def staged(c):
            return zc(c + IN_Z // 2)

        (B1, B2, B3, G1, T1, G2, T2, G3, T3, BIAS1, BIAS2, BIAS3, EPSC, MEAN, VAR, MEANC, DEV, DEV2, Q, VARC, STD,
         RSTD, SCALE, MS, SHIFT, SCALE3, SHIFT3) = range(27)

        def v(i, n=1):
            return vec[:, i:i + n]

        weights_in = sem("weights_in")
        edges_in = [sem(f"edges_in{i}") for i in range(2)]
        x_in = [sem(f"x_in{i}") for i in range(4)]
        table_zeroed = sem("table_zeroed")
        rows_added = sem("rows_added")
        parked_out = [sem(f"parked_out{i}") for i in range(2)]
        parked_in = sem("parked_in")
        sums_in = [sem(f"sums_in{i}") for i in range(4)]
        W3_in = sem("W3_in")
        x_again = [sem(f"x_again{i}") for i in range(3)]
        out_stored = sem("out_stored")
        consts = sem("consts")
        fconst = sem("fconst")
        shared_ready = sem("shared_ready")
        bias1_ready = sem("bias1_ready")
        high_ready = sem("high_ready")
        rest_ready = sem("rest_ready")
        mid_ready = sem("mid_ready")
        low_ready = sem("low_ready")
        srcf_ready = sem("srcf_ready")
        sel_ready = sem("sel_ready")
        upto_ready = sem("upto_ready")
        target_steps = sem("target_steps")
        target_ready = sem("target_ready")
        summed = sem("summed")
        sums_copied = sem("sums_copied")
        y_ready = sem("y_ready")
        rows_ready = sem("rows_ready")
        ln_steps = sem("ln_steps")
        var_ready = sem("var_ready")
        std_ready = sem("std_ready")
        rstd_ready = sem("rstd_ready")
        norm_ready = sem("norm_ready")
        h_ready = sem("h_ready")
        hT_ready = sem("hT_ready")
        hT_kept = sem("hT_kept")
        floor_ready = sem("floor_ready")
        inv_ready = sem("inv_ready")
        means_ready = sem("means_ready")
        meansT_ready = sem("meansT_ready")
        meansT_kept = sem("meansT_kept")
        a1_ready = sem("a1_ready")
        added = sem("added")
        z1_ready = sem("z1_ready")
        z1_seen = sem("z1_seen")
        a_ready = [sem(f"a{i}_ready") for i in (2, 3)]
        z_ready = [sem(f"z{i}_ready") for i in (2, 3)]
        z_seen = [sem(f"z{i}_seen") for i in (2, 3)]
        fold_pe = sem("fold_pe")
        fold_dve = sem("fold_dve")
        fold_act = sem("fold_act")
        affine_ready = sem("affine_ready")
        zT_ready = sem("zT_ready")
        out_ready = sem("out_ready")

        FOLD = [3 + 12 * layer for layer in range(3)]
        MEAN_READY = [f + 1 for f in FOLD]
        Q_READY = [f + 5 for f in FOLD]
        VAR_READY = [f + 6 for f in FOLD]
        SHIFT_READY = [f + 10 for f in FOLD]
        BIAS_READY = [f + 11 for f in FOLD]
        WEIGHTS_READY = [f + 12 for f in FOLD]

        SELS = H + G
        ADDED = 16 * G

        weight_loads = []
        for h in range(2):
            q = slice(h * D, (h + 1) * D)
            weight_loads += [(Wa[q, q], W1[0:D, :]), (Wb[q, q], W2[:, :]), (W1b_hm[q, 0:D], W1[D:2 * D, :]),
                             (W1c2[0:D, q], W1[2 * D:3 * D, :])]
            for i, a in ((B1, b1), (B2, b2), (B3, b3), (G1, g1), (T1, bt1), (G2, g2), (T2, bt2), (G3, g3), (T3, bt3)):
                weight_loads.append((vec[q, i:i + 1], a.rearrange("(p a) -> p a", a=1)))
        weight_loads += [(W1b_lo[0:D, 0:D], W1[D:2 * D, :]), (g0[0:D, :], global_attr[0:1, :].rearrange("a p -> p a"))]

        def tiles_of(h):
            return [(j, max(0, j - H * h)) for j in range(H * (h + 1))]

        BANKS = (0, 1, 2, 5)

        block = ctx.enter_context(nc.Block())

        @block.sync
        def _(sp):
            def load_edges(g, b, free, tail=False):
                if free:
                    sp.wait_ge(sel_ready, SELS * (g - 1))
                    nc.sync.nop(nofuse=True)
                    sp.wait_ge(srcf_ready, g - 1)
                    nc.sync.nop(nofuse=True)
                    sp.wait_ge(rest_ready, 2 * (g - 1))
                    nc.sync.nop(nofuse=True)
                n = EP if tail else P
                e = slice(EFULL * EG, NE) if tail else bass.ds(g * EG, EG)
                sp.dma_start(srci[b][0:n, :], src[e].rearrange("(p j) -> p j", j=G)).then_inc(edges_in[b], 16)
                sp.dma_start(ids[b][0:n, 0:n * G], src[e].rearrange("(a e) -> a e", a=1).broadcast_to([n, n * G])
                             ).then_inc(edges_in[b], 16)
                sp.dma_start(edges[b][0:n, :], edge_attr[e, :].rearrange("(p j) c -> p (j c)", j=G)
                             ).then_inc(edges_in[b], 16)

            def load_x(c, slot, free, tail=False):
                if free:
                    sp.wait_ge(h_ready, c - 3)
                    nc.sync.nop(nofuse=True)
                n, k = (TP, TG) if tail else (P, NG)
                sp.dma_start(wk(slot)[0:n, 0:k * D], nodes_of(x, c, tail)).then_inc(x_in[slot], 16)

            def park(c, b, tail=False):
                sp.wait_ge(hT_kept, c + 1)
                nc.sync.nop(nofuse=True)
                if tail:
                    sp.dma_start(parked_tail, park_tile[b][:, 0:TCOLS]).then_inc(parked_out[b], 16)
                else:
                    sp.dma_start(parked[bass.ds((c - IN_Z) * P, P), :], park_tile[b]).then_inc(parked_out[b], 16)

            def load_ahead(c, slot):
                sp.dma_start(staged(c), nodes_of(x, c)).then_inc(x_in[slot], 16)

            for c in range(4):
                load_ahead(c, c)
            with sp.Fori(1, AHEAD // 4) as k:
                for i in range(4):
                    sp.wait_ge(x_in[i], 16 * k)
                    nc.sync.nop(nofuse=True)
                    load_ahead(4 * k + i, i)
            load_edges(0, 0, False)
            load_edges(1, 1, False)
            for c in range(2):
                sp.wait_ge(x_in[c], 16 * (AHEAD // 4))
                load_x(AHEAD + c, c, False)

            def step(k, i, parks=False, loads=True):
                if loads:
                    load_x(4 * k + i + AHEAD + 2, (i + 2) % 4, True)
                if i % 2 == 0:
                    load_edges(2 * k + i // 2 + 1, (i // 2 + 1) % 2, True)
                if parks:
                    park(4 * k + i + AHEAD - 2, i % 2)

            for i in range(4):
                if i == 0:
                    load_x(AHEAD + 2, 2, True)
                else:
                    step(0, i)
            with sp.Fori(1, PARK) as k:
                for i in range(4):
                    step(k, i)
            with sp.Fori(PARK, XEND - 1) as k:
                for i in range(4):
                    step(k, i, parks=True)
            for i in range(2):
                step(XEND - 1, i, parks=True)
            load_x(FULL - 1, 0, True)
            load_edges(2 * XEND, 0, True)
            park(FULL - 5, 0)
            load_x(FULL, 1, True, tail=True)
            park(FULL - 4, 1)
            for i in range(3):
                step(XEND, i, parks=True, loads=False)
            park(FULL, 1, tail=True)
            with sp.Fori(XEND + 1, LOOPS - 1) as k:
                for i in range(4):
                    step(k, i, loads=False)
            step(LOOPS - 1, 0, loads=False)
            load_edges(EFULL, 0, True, tail=True)

            def load_sums(c, r, free, tail=False):
                if free:
                    sp.wait_ge(meansT_ready, c - 3)
                n, k = (TP, TG) if tail else (P, NG)
                sp.dma_start(wk(r)[0:n, 0:k * ROW], nodes_of(table, c, tail)).then_inc(sums_in[r], 16)

            sp.wait_ge(h_ready, NC)
            sp.wait_ge(rows_added, 16 * G * NGR)
            for r in range(4):
                load_sums(r, r, False)
            sp.wait_ge(hT_kept, NC)
            for b in range(2):
                sp.wait_ge(parked_out[b], 16 * ((NC - IN_Z) // 2 + (b == 1) * ((NC - IN_Z) % 2)))
            sp.dma_start(Z[:, FULL * COLS:HALF], parked_tail).then_inc(parked_in, 16)

            def unpark(i):
                sp.dma_start(zc(IN_Z + i), parked[bass.ds(i * P, P), :]).then_inc(parked_in, 16)

            if LATE % 2:
                unpark(0)
            with sp.Fori(1, 1 + LATE // 2) as k:
                for i in range(4):
                    load_sums(4 * k + i, i, True)
                    if i % 2:
                        unpark(LATE % 2 + 2 * k - 2 + i // 2)
            with sp.Fori(1 + LATE // 2, FULL // 4) as k:
                for i in range(4):
                    load_sums(4 * k + i, i, True)
            load_sums(FULL - 1, 0, True)
            load_sums(FULL, 1, True, tail=True)

            sp.wait_ge(z1_seen, NC)
            for h in range(2):
                sp.dma_start(Wa[h * D:(h + 1) * D, h * D:(h + 1) * D], W3[:, :]).then_inc(W3_in, 16)

            def reload_x(c, s, free, tail=False):
                if free:
                    sp.wait_ge(out_ready, c - 2)
                n, k = (TP, TG) if tail else (P, NG)
                sp.dma_start(wk(s)[0:n, 0:k * D], nodes_of(x, c, tail)).then_inc(x_again[s], 16)

            def store(c, tail=False):
                sp.wait_ge(out_ready, c + 1)
                n = TP if tail else P
                k = TG if tail else NG
                sp.dma_start(nodes_of(out, c, tail), wk(FULL % 3)[0:n, 0:k * D] if tail else zc(c)
                             ).then_inc(out_stored, 16)

            for c in range(3):
                reload_x(c, c, False)
            with sp.Fori(0, (FULL - 4) // 3) as k:
                for s in range(3):
                    store(3 * k + s)
                    reload_x(3 * k + s + 3, s, True)
            for c in range(FULL - 4, NC):
                store(c, tail=(c == FULL))
                if c + 3 < NC:
                    reload_x(c + 3, c % 3, True, tail=(c + 3 == FULL))
            sp.wait_ge(out_stored, 16 * NC)

        @block.gpsimd
        def _(pool):
            nc.gpsimd.memset(zero, 0.0).then_inc(consts, 1)
            nc.gpsimd.memset(Wa[:, :], 0.0).then_inc(consts, 1)
            nc.gpsimd.memset(Wb[:, :], 0.0).then_inc(consts, 1)
            nc.gpsimd.memset(W1b_hm, 0.0).then_inc(consts, 1)
            nc.gpsimd.memset(W1b_lo, 0.0).then_inc(consts, 1)
            nc.gpsimd.memset(v(EPSC), EPS).then_inc(consts, 1)
            nc.gpsimd.memset(ident[:, :], 0.0).then_inc(consts, 1)
            nc.gpsimd.memset(upto, 1.0).then_inc(consts, 1)
            nc.gpsimd.memset(pick[:, 0:ROW], 0.0).then_inc(fconst, 1)
            nc.gpsimd.memset(pick[:, ROW:LOW], 1.0).then_inc(fconst, 1)
            for b in range(2):
                nc.gpsimd.memset(low_one[b][:, :, D:ROW], 1.0).then_inc(fconst, 1)
                nc.gpsimd.memset(low_one[b][:, :, ROW:LOW], 0.0).then_inc(fconst, 1)
                nc.gpsimd.memset(seen0[b], 0.0).then_inc(fconst, 1)
            nc.gpsimd.iota(spare_i, pattern=[[P, G]], base=N, channel_multiplier=1).then_inc(fconst, 1)
            pool.wait_ge(consts, 8)
            nc.gpsimd.affine_select(out=ident[:, :], in_=ident[:, :], compare_op=ALU.not_equal, fill=1.0, base=0,
                                    pattern=[[-1, P]], channel_multiplier=1).then_inc(fconst, 1)
            nc.gpsimd.affine_select(out=upto[:, 0, :], in_=upto[:, 0, :], compare_op=ALU.is_ge, fill=0.0, base=0,
                                    pattern=[[1, P]], channel_multiplier=-1).then_inc(fconst, 1)
            pool.wait_ge(fconst, 11)
            nc.gpsimd.tensor_copy(W1b_lo[D:P, D:LOW], ident[D:P, D:LOW]).then_inc(fconst, 1)
            for dst, a in weight_loads:
                pool.dma_start(dst, a).then_inc(weights_in, 16)

            def low(g, b, h, free, tail=False):
                n = EP if tail else P
                s = 2 * g + h
                q = slice(h * H, (h + 1) * H)
                pool.wait_ge(mid_ready, s + 1)
                if free:
                    pool.wait_ge(summed, s - 3)
                nc.gpsimd.tensor_tensor(low_one[b][0:n, q, 0:D], rest[h][0:n, :].rearrange("p (j c) -> p j c", j=H),
                                        high_mid[b][0:n, q, D:P], ALU.subtract).then_inc(low_ready, 1)

            for g in range(2):
                for h in range(2):
                    low(g, g, h, False)
            pool.wait_ge(table_zeroed, 16 * GRAINS)

            def scatter(g, b, tail=False, after=None):
                n = EP if tail else P
                pool.wait_ge(rows_ready, 2 * g + 2)
                pool.wait_ge(target_ready, g + 1)
                pool.wait_ge(rows_added, ADDED * g)
                nc.gpsimd.nop(nofuse=True)
                for j in range(G):
                    nc.gpsimd.indirect_dma_start(
                        out=table, out_offset=bass.IndirectOffsetOnAxis(ap=target[b][0:n, j:j + 1], axis=0),
                        in_=rows[b][0:n, j * LOW:j * LOW + ROW], in_offset=None,
                        compute_op=ALU.add).then_inc(rows_added, 16)
                    if j == LOW_AT and after is not None:
                        after()

            def pair(k, last=False):
                for b in range(2):
                    if last and b == 1:
                        scatter(2 * k + b, b)
                        continue
                    scatter(2 * k + b, b, after=lambda: low(2 * k + b + 2, b, 0, True, last))
                    low(2 * k + b + 2, b, 1, True, last)

            pair(0)
            with pool.Fori(1, LOOPS - 1) as k:
                pair(k)
            pair(LOOPS - 1, last=True)
            scatter(EFULL, 0, tail=True)

            def means(c, r, tail=False):
                n, k = (TP, TG) if tail else (P, NG)
                pool.wait_ge(inv_ready, c + 1)
                nc.gpsimd.tensor_tensor(
                    wk(r)[0:n, 0:k * D].rearrange("p (g c) -> p g c", c=D),
                    wk(r)[0:n, 0:k * ROW].rearrange("p (g c) -> p g c", c=ROW)[:, :, 0:D],
                    sm(4 + r, n, k).rearrange("p (g c) -> p g c", c=1).broadcast_to([n, k, D]),
                    ALU.mult).then_inc(means_ready, 1)

            with pool.Fori(0, FULL // 4) as k:
                for i in range(4):
                    means(4 * k + i, i)
            means(FULL - 1, 0)
            means(FULL, 1, tail=True)

        @block.vector
        def _(dve):
            def same_node(s, g, b, h, k, first, between, tail=False):
                n = EP if tail else P
                if not first:
                    dve.wait_ge(summed, s - 1)
                dve.wait_ge(srcf_ready, g + 1)
                cols = ids[b][0:n, 0:n * G].rearrange("q (p i) -> q i p", i=G)
                count = seen0[b] if h == 0 else seen1[b]
                for j, first_col in tiles_of(h):
                    nc.vector.tensor_scalar(
                        sel[h][0:n, j, first_col * n:H * n].rearrange("q (i p) -> q i p", p=n),
                        cols[:, H * h + first_col:H * (h + 1), :], srcf[b][0:n, j:j + 1], 0.0, ALU.is_equal, ALU.add,
                        accum_out=count[0:n, j:j + 1]).then_inc(sel_ready, 1)
                    for part in between[j]:
                        part()

            def float_ids(g, b, use, free, tail=False):
                n = EP if tail else P
                dve.wait_ge(edges_in[b], 48 * (use + 1))
                if free:
                    dve.wait_ge(target_ready, g - 1)
                nc.vector.tensor_copy(srcf[b][0:n, :], srci[b][0:n, :]).then_inc(srcf_ready, 1)

            def own_tile(s, g, h, tail=False):
                n = EP if tail else P
                dve.wait_ge(sel_ready, SELS * g + (H if h == 0 else SELS))
                blocks = sel[h].rearrange("p j e -> p (j e)")[0:n, H * h * H * P:]
                a = diag_view(blocks, n)
                nc.vector.tensor_tensor(sel_upto[h][0:n, :, 0:n], a, upto[0:n, :, 0:n].broadcast_to([n, H, n]),
                                        ALU.mult).then_inc(upto_ready, 1)

            def diag_view(blocks, n):
                return bass.AP(blocks.tensor, blocks.offset, [blocks.ap[0], [H * P + n, H], [1, n]])

            def edge_rest(s, b, h, free, tail=False):
                n = EP if tail else P
                q = slice(h * H, (h + 1) * H)
                dve.wait_ge(high_ready, s + 1)
                if free:
                    dve.wait_ge(low_ready, s - 1)
                nc.vector.tensor_tensor(rest[h][0:n, :].rearrange("p (j c) -> p j c", j=H),
                                        edges[b][0:n, :].rearrange("p (j c) -> p j c", j=G)[:, q, :],
                                        high_mid[b][0:n, q, 0:D], ALU.subtract).then_inc(rest_ready, 1)

            TS = 4

            def targets(g, b, free, tail=False):
                n = EP if tail else P

                def gap_and_seen():
                    nc.vector.tensor_tensor(gap[0:n, :], spare[0:n, :], srcf[b][0:n, :],
                                            ALU.subtract).then_inc(target_steps, 1)
                    nc.vector.tensor_tensor(seen[0:n, :], seen0[b][0:n, :], seen1[b][0:n, :],
                                            ALU.add).then_inc(target_steps, 1)

                def later_ones():
                    dve.wait_ge(rows_ready, 2 * g + 2)
                    dve.wait_ge(target_steps, TS * g + 2)
                    nc.vector.tensor_tensor(later[0:n, :], seen[0:n, :], rows[b][0:n, :].rearrange(
                        "p (j c) -> p j c", c=LOW)[:, :, ROW], ALU.subtract).then_inc(target_steps, 1)

                def mask():
                    dve.wait_ge(target_steps, TS * g + 3)
                    nc.vector.scalar_tensor_tensor(out=masked[0:n, :], in0=later[0:n, :], scalar=1.0, in1=gap[0:n, :],
                                                   op0=ALU.min, op1=ALU.mult).then_inc(target_steps, 1)

                def place():
                    dve.wait_ge(target_steps, TS * g + 4)
                    if free:
                        dve.wait_ge(rows_added, ADDED * (g - 1))
                    nc.vector.tensor_tensor(target[b][0:n, :], masked[0:n, :], srcf[b][0:n, :],
                                            ALU.add).then_inc(target_ready, 1)

                return [gap_and_seen, later_ones, mask, place]

            LN = NG + 3

            def sums_and_spreads(b, n, q):
                return small[0:n, NSUM + 2 * b:NSUM + 2 * b + 2, :].rearrange("p r g -> p (r g)")[:, 0:2 * q].rearrange(
                    "p (g s) -> p g s", s=2)

            def ln_stats(c, b, slot, use, tail=False, tile=None):
                n, q = (TP, TG) if tail else (P, NG)
                dve.wait_ge(x_in[slot], 16 * (use + 1))
                tile = wk(slot) if tile is None else tile
                for g in range(q):
                    nc.vector.bn_stats(stats_x[b][0:n, g * 6:(g + 1) * 6], tile[0:n, g * D:(g + 1) * D]
                                       ).then_inc(ln_steps, 1 + (NG - q) * (g == 0))

            def ln_sums(c, b, tail=False):
                n, q = (TP, TG) if tail else (P, NG)
                st = stats_x[b][0:n, 0:q * 6].rearrange("p (g s) -> p g s", s=6)
                dve.wait_ge(ln_steps, LN * c + NG)
                nc.vector.tensor_tensor(sm(DIFF, n, q), st[:, :, 1], st[:, :, 4], ALU.subtract).then_inc(ln_steps, 1)
                nc.vector.tensor_tensor(sums_and_spreads(b, n, q), st[:, :, 1:3], st[:, :, 4:6],
                                        ALU.add).then_inc(ln_steps, 1)

            def ln_square(c, b, tail=False):
                n, q = (TP, TG) if tail else (P, NG)
                dve.wait_ge(ln_steps, LN * c + NG + 2)
                nc.vector.tensor_tensor(sm(DIFF2, n, q), sm(DIFF, n, q), sm(DIFF, n, q), ALU.mult).then_inc(ln_steps, 1)

            def ln_var(c, b, tail=False):
                n, q = (TP, TG) if tail else (P, NG)
                dve.wait_ge(ln_steps, LN * c + NG + 3)
                nc.vector.scalar_tensor_tensor(out=sm(NVAR + b, n, q), in0=sm(DIFF2, n, q), scalar=D / 4.0,
                                               in1=sums_and_spreads(b, n, q)[:, :, 1], op0=ALU.mult,
                                               op1=ALU.add).then_inc(var_ready, 1)

            def ln_rstd(c, b, free, tail=False):
                n, q = (TP, TG) if tail else (P, NG)
                dve.wait_ge(std_ready, c + 1)
                if free:
                    dve.wait_ge(h_ready, c - 1)
                nc.vector.reciprocal(sm(NRSTD + b, n, q), sm(NSTD + b, n, q)).then_inc(rstd_ready, 1)

            def ln_shift(c, b, tail=False):
                n, q = (TP, TG) if tail else (P, NG)
                dve.wait_ge(rstd_ready, c + 1)
                nc.vector.scalar_tensor_tensor(out=sm(NSHIFT + b, n, q), in0=sums_and_spreads(b, n, q)[:, :, 0],
                                               scalar=-0.5, in1=sm(NRSTD + b, n, q), op0=ALU.mult,
                                               op1=ALU.mult).then_inc(norm_ready, 1)

            dve.wait_ge(fconst, 12)
            nc.vector.tensor_copy(spare, spare_i).then_inc(fconst, 1)
            dve.wait_ge(fconst, 13)

            def x_only(k, i, first=False):
                c = 4 * k + i
                if not first:
                    ln_rstd(c - 1, (i + 1) % 2, i > 2 or not isinstance(k, int))
                ln_stats(c, i % 2, i, k, tile=staged(c))
                if not first:
                    ln_shift(c - 1, (i + 1) % 2)
                ln_sums(c, i % 2)
                ln_square(c, i % 2)
                ln_var(c, i % 2)

            x_only(0, 0, True)
            for i in range(1, 4):
                x_only(0, i)
            with dve.Fori(1, AHEAD // 4) as k:
                for i in range(4):
                    x_only(k, i)
            dve.wait_ge(shared_ready, 1)
            nc.vector.tensor_tensor(v(BIAS1), v(B1), ps[:, 5, 500:501], ALU.add).then_inc(bias1_ready, 1)
            float_ids(0, 0, 0, False)
            edge_rest(0, 0, 0, False)

            def step(k, i, x=True, x_before=True, first=False, tail=False, next_tail=False, last=False, x_tail=False,
                     before_tail=False):
                s, g, h, b = 4 * k + i, 2 * k + i // 2, i % 2, i // 2
                c, cb, u = s + AHEAD, i % 2, k + AHEAD // 4
                if x:
                    ln_stats(c, cb, i, u, x_tail)
                between = [[] for _ in range(G)]
                if x:
                    for j, part in enumerate((ln_sums, ln_square, ln_var)):
                        between[j].append(lambda part=part: part(c, cb, x_tail))
                if h == 1 and not (first and i < 4):
                    for j, part in enumerate(targets(g - 1, 1 - b, not first)):
                        between[j + TARGETS_AT].append(part)
                if x_before:
                    between[2].append(lambda: ln_rstd(c - 1, 1 - cb, True, before_tail))
                    between[3].append(lambda: ln_shift(c - 1, 1 - cb, before_tail))
                if first and i == 2:
                    between[3] += targets(0, 0, False)
                same_node(s, g, b, h, k, first and i < 2, between, tail)
                own_tile(s, g, h, tail)
                if h == 1 and not last:
                    float_ids(g + 1, 1 - b, k + b, not (first and b == 0), next_tail)
                if not last:
                    edge_rest(s + 1, ((i + 1) // 2) % 2, 1 - h, not (first and i == 0), next_tail)

            for i in range(4):
                step(0, i, first=True)
            with dve.Fori(1, XEND) as k:
                for i in range(4):
                    step(k, i)
            step(XEND, 0)
            step(XEND, 1, x_tail=True)
            step(XEND, 2, x=False, before_tail=True)
            step(XEND, 3, x=False, x_before=False)
            with dve.Fori(XEND + 1, LOOPS - 1) as k:
                for i in range(4):
                    step(k, i, x=False, x_before=False)
            for i in range(4):
                step(LOOPS - 1, i, x=False, x_before=False, next_tail=(i == 3))
            step(LOOPS, 0, x=False, x_before=False, tail=True, next_tail=True)
            step(LOOPS, 1, x=False, x_before=False, tail=True, last=True)
            for part in targets(EFULL, 0, True, tail=True):
                part()

            dve.wait_ge(hT_ready, NC)
            dve.wait_ge(h_ready, NC)

            def floor(c, r, use, tail=False):
                n, q = (TP, TG) if tail else (P, NG)
                dve.wait_ge(sums_in[r], 16 * (use + 1))
                cnt = wk(r)[0:n, 0:q * ROW].rearrange("p (g c) -> p g c", c=ROW)[:, :, D]
                nc.vector.tensor_scalar(sm(r, n, q), cnt, 1.0, None, ALU.max).then_inc(floor_ready, 1)

            def inverse(c, r, free, tail=False):
                n, q = (TP, TG) if tail else (P, NG)
                dve.wait_ge(floor_ready, c + 1)
                if free:
                    dve.wait_ge(means_ready, c - 3)
                nc.vector.reciprocal(sm(4 + r, n, q), sm(r, n, q)).then_inc(inv_ready, 1)

            def add(c, r, tail=False):
                w = TCOLS if tail else COLS
                dve.wait_ge(a1_ready, c + 1)
                dve.wait_ge(meansT_kept, c + 1)
                nc.vector.tensor_tensor(zc(c, tail), ps[:, BANKS[r], 0:w], zc(c, tail), ALU.add).then_inc(added, 1)

            def see(k, b, ready, seen_sem, tail=False):
                c = 2 * k + b
                dve.wait_ge(ready, c + 1)
                nc.vector.bn_stats(ps[:, 6 + b, bass.ds(k * 6, 6)], zc(c, tail)).then_inc(seen_sem, 1)

            def layer1(k, i, first=False, see_one=True, tail=False, next_tail=False):
                c = 4 * k + i
                inverse(c, i, not (first and i < 4), tail)
                if not (first and i < 2):
                    add(c - 2, (i - 2) % 4)
                if not tail:
                    floor(c + 1, (i + 1) % 4, k + (i + 1) // 4, next_tail)
                if see_one and not first:
                    see(2 * k + (i - 5) // 2, (i - 5) % 2, z1_ready, z1_seen)

            floor(0, 0, 0)
            for i in range(4):
                layer1(0, i, first=True)
            layer1(1, 0, see_one=False)
            for i in range(1, 4):
                layer1(1, i)
            with dve.Fori(2, FULL // 4) as k:
                for i in range(4):
                    layer1(k, i)
            layer1(FULL // 4, 0, next_tail=True)
            layer1(FULL // 4, 1, tail=True)
            add(FULL - 1, (FULL - 1) % 4)
            see(PAIRS - 2, 1, z1_ready, z1_seen)
            add(FULL, FULL % 4, tail=True)
            see(PAIRS - 1, 0, z1_ready, z1_seen)
            see(PAIRS - 1, 1, z1_ready, z1_seen)
            see(PAIRS, 0, z1_ready, z1_seen)
            see(PAIRS, 1, z1_ready, z1_seen, tail=True)

            done = [0]

            def chain(ins):
                done[0] += 1
                ins.then_inc(fold_dve, 1)
                dve.wait_ge(fold_dve, done[0])

            def fold(layer, seen_sem, gi, ti, scale, shift):
                dve.wait_ge(seen_sem, NC)
                chain(nc.vector.bn_aggr(v(MEAN, 2), ps[:, 6:8, 0:3 * NC]))
                dve.wait_ge(fold_pe, 3 * layer + 1)
                chain(nc.vector.tensor_copy(v(MEANC), ps[:, 5, 0:1]))
                chain(nc.vector.tensor_tensor(v(DEV), v(MEAN), v(MEANC), ALU.subtract))
                chain(nc.vector.tensor_tensor(v(DEV2), v(DEV), v(DEV), ALU.mult))
                chain(nc.vector.tensor_tensor(v(Q), v(DEV2), v(VAR), ALU.add))
                dve.wait_ge(fold_pe, 3 * layer + 2)
                chain(nc.vector.tensor_copy(v(VARC), ps[:, 5, 1:2]))
                dve.wait_ge(fold_act, layer + 1)
                chain(nc.vector.reciprocal(v(RSTD), v(STD)))
                chain(nc.vector.tensor_tensor(v(scale), v(gi), v(RSTD), ALU.mult))
                chain(nc.vector.tensor_tensor(v(MS), v(MEANC), v(scale), ALU.mult))
                chain(nc.vector.tensor_tensor(v(shift), v(ti), v(MS), ALU.subtract))

            def average():
                chain(nc.vector.tensor_tensor(wk(4)[:, P:P + D], ident[:, 0:D], ident[:, D:P], ALU.add))
                for h in range(2):
                    chain(nc.vector.tensor_scalar(wk(4)[:, h * D:(h + 1) * D], wk(4)[:, P:P + D], 0.5, None, ALU.mult))

            average()
            fold(0, z1_seen, G1, T1, SCALE, SHIFT)
            dve.wait_ge(fold_pe, 3)
            chain(nc.vector.tensor_tensor(v(BIAS2), ps[:, 5, 2:3], v(B2), ALU.add))
            chain(nc.vector.tensor_scalar(Wb[:, :], Wb[:, :], v(SCALE), None, ALU.mult))

            for layer in (1, 2):
                ready, seen_sem = z_ready[layer - 1], z_seen[layer - 1]
                with dve.Fori(0, PAIRS) as k:
                    for b in range(2):
                        see(k, b, ready, seen_sem)
                see(PAIRS, 0, ready, seen_sem)
                see(PAIRS, 1, ready, seen_sem, tail=True)
                if layer == 1:
                    fold(1, seen_sem, G2, T2, SCALE, SHIFT)
                    dve.wait_ge(fold_pe, 6)
                    chain(nc.vector.tensor_tensor(v(BIAS3), ps[:, 5, 2:3], v(B3), ALU.add))
                    chain(nc.vector.tensor_scalar(Wa[:, :], Wa[:, :], v(SCALE), None, ALU.mult))
                else:
                    fold(2, seen_sem, G3, T3, SCALE3, SHIFT3)

            def finish(c, b, s, use, tail=False):
                n, w = (TP, TG * D) if tail else (P, COLS)
                dve.wait_ge(x_again[s], 16 * (use + 1))
                dve.wait_ge(zT_ready, c + 1)
                o = wk(s)[0:n, 0:w] if tail else zc(c)
                nc.vector.tensor_tensor(o, ps[0:n, b, 0:w], wk(s)[0:n, 0:w], ALU.add).then_inc(out_ready, 1)

            with dve.Fori(0, FULL // 6) as k:
                for i in range(6):
                    finish(6 * k + i, i % 2, i % 3, 2 * k + i // 3)
            for c in range(FULL // 6 * 6, NC):
                finish(c, c % 2, c % 3, c // 3, tail=(c == FULL))

        @block.scalar
        def _(act):
            act.wait_ge(consts, 8)

            def high(s, b, h, k, free, tail=False):
                n = EP if tail else P
                q = slice(h * H, (h + 1) * H)
                act.wait_ge(edges_in[b], 48 * (k + 1))
                if free:
                    act.wait_ge(summed, s - 2 - h)
                nc.scalar.copy(high_mid[b][0:n, q, 0:D],
                               edges[b][0:n, :].rearrange("p (j c) -> p j c", j=G)[:, q, :]).then_inc(high_ready, 1)

            def mid(s, b, h, tail=False):
                n = EP if tail else P
                act.wait_ge(rest_ready, s + 1)
                nc.scalar.copy(high_mid[b][0:n, h * H:(h + 1) * H, D:P],
                               rest[h][0:n, :].rearrange("p (j c) -> p j c", j=H)).then_inc(mid_ready, 1)

            def sums(s, h, tail=False):
                w = (EP if tail else P) * H
                act.wait_ge(summed, s + 1)
                act.wait_ge(y_ready, s)
                nc.scalar.copy(sums_hm[:, 0:w], ps[:, h, 0:w]).then_inc(sums_copied, 1)
                nc.scalar.copy(sums_lo[0:LOW, 0:w], ps[0:LOW, 2 + h, 0:w]).then_inc(sums_copied, 1)

            def row(s, g, b, h, free, tail=False):
                n = EP if tail else P
                act.wait_ge(y_ready, s + 1)
                if free:
                    act.wait_ge(rows_added, ADDED * (g - 1))
                nc.scalar.copy(rows[b][0:n, h * H * LOW:(h + 1) * H * LOW],
                               ps[0:n, 4 + h, 0:H * LOW]).then_inc(rows_ready, 1)

            def std(c, b, tail=False):
                n, q = (TP, TG) if tail else (P, NG)
                act.wait_ge(var_ready, c + 1)
                nc.scalar.activation(sm(NSTD + b, n, q), sm(NVAR + b, n, q), ACT.Sqrt, bias=v(EPSC)[0:n, :],
                                     scale=1.0 / D).then_inc(std_ready, 1)

            def normed(c, b, slot, free, tail=False, tile=None):
                n, q = (TP, TG) if tail else (P, NG)
                act.wait_ge(norm_ready, c + 1)
                if free:
                    act.wait_ge(hT_ready, c - 1)
                tile = wk(slot) if tile is None else tile
                for g in range(q):
                    ins = nc.scalar.activation(h_tile[b][0:n, g * D:(g + 1) * D], tile[0:n, g * D:(g + 1) * D],
                                               ACT.Relu, bias=small[0:n, NSHIFT + b, g:g + 1],
                                               scale=small[0:n, NRSTD + b, g:g + 1])
                ins.then_inc(h_ready, 1)

            def keep(c, b, dst, wait=None, tail=False):
                w = TCOLS if tail else COLS
                act.wait_ge(hT_ready, c + 1)
                if wait is not None:
                    act.wait_ge(parked_out[b], wait)
                nc.scalar.copy(dst[:, 0:w], ps[:, 6 + b, 0:w]).then_inc(hT_kept, 1)

            def x_only(k, i, first=False):
                c = 4 * k + i
                std(c, i % 2)
                if not (first and i < 1):
                    normed(c - 1, (i + 1) % 2, (i + 3) % 4, not (first and i < 3), tile=staged(c - 1))
                if not (first and i < 2):
                    keep(c - 2, i % 2, zc(c - 2))

            def clear(first, n):
                for j in range(n):
                    act.dma_start(table_by_partition[:, bass.ds(first + j, 1), :].rearrange("p n c -> p (n c)"),
                                  zero).then_inc(table_zeroed, 16)

            for i in range(4):
                clear(i * FIRST_CLEARS, FIRST_CLEARS)
                x_only(0, i, first=True)
            with act.Fori(1, AHEAD // 4) as k:
                for i in range(4):
                    clear(4 * FIRST_CLEARS - 4 * CLEARS + (4 * k + i) * CLEARS, CLEARS)
                    x_only(k, i)
            high(0, 0, 0, 0, False)

            def step(k, i, x=True, x_before=True, where="Z", first=False, tail=False, next_tail=False, last=False,
                     x_tail=False, before_tail=False, kept_tail=False):
                s, g, h, b = 4 * k + i, 2 * k + i // 2, i % 2, i // 2
                c, cb = s + AHEAD, i % 2
                mid(s, b, h, tail)
                if not last:
                    high(s + 1, ((i + 1) % 4) // 2, 1 - h, k + (i == 3), not (first and i < 3), next_tail)
                if not (first and i == 0):
                    sums(s - 1, 1 - h, tail and h == 1)
                if where == "Z":
                    keep(c - 2, cb, zc(c - 2))
                elif where is not None:
                    keep(c - 2, cb, park_tile[cb], 16 * (2 * (k - PARK) + i // 2) if where == "DRAM" else None,
                         kept_tail)
                if x_before:
                    normed(c - 1, 1 - cb, (i + 3) % 4, True, before_tail,
                           staged(AHEAD - 1) if first and i == 0 else None)
                if x:
                    std(c, cb, x_tail)
                if not (first and i == 0):
                    pb = ((i + 3) % 4) // 2
                    row(s - 1, 2 * k + (i - 1) // 2, pb, 1 - h, not first, tail and h == 1)

            for i in range(4):
                clear(GRAINS + (i - 4) * LAST_CLEARS, LAST_CLEARS)
                step(0, i, first=True)
            with act.Fori(1, PARK) as k:
                for i in range(4):
                    step(k, i)
            for i in range(4):
                step(PARK, i, where="park" if i < 2 else "DRAM")
            with act.Fori(PARK + 1, XEND) as k:
                for i in range(4):
                    step(k, i, where="DRAM")
            step(XEND, 0, where="DRAM")
            step(XEND, 1, where="DRAM", x_tail=True)
            step(XEND, 2, x=False, where="DRAM", before_tail=True)
            step(XEND, 3, x=False, x_before=False, where="DRAM", kept_tail=True)
            with act.Fori(XEND + 1, LOOPS - 1) as k:
                for i in range(4):
                    step(k, i, x=False, x_before=False, where=None)
            for i in range(4):
                step(LOOPS - 1, i, x=False, x_before=False, where=None, next_tail=(i == 3))
            step(LOOPS, 0, x=False, x_before=False, where=None, tail=True, next_tail=True)
            step(LOOPS, 1, x=False, x_before=False, where=None, tail=True, last=True)
            sums(STEPS - 1, 1, tail=True)
            row(STEPS - 1, EFULL, 0, 1, True, tail=True)

            def keep_means(c, b, tail=False):
                w = TCOLS if tail else COLS
                act.wait_ge(meansT_ready, c + 1)
                act.wait_ge(a1_ready, c + 1)
                nc.scalar.copy(zc(c, tail), ps[:, 3 + b, 0:w]).then_inc(meansT_kept, 1)

            def relu1(c, tail=False):
                act.wait_ge(added, c + 1)
                nc.scalar.activation(zc(c, tail), zc(c, tail), ACT.Relu, bias=v(BIAS1)).then_inc(z1_ready, 1)

            act.wait_ge(bias1_ready, 1)
            for c in range(4):
                keep_means(c, c % 2)
            relu1(0)
            with act.Fori(2, PAIRS) as k:
                keep_means(2 * k, 0)
                relu1(2 * k - 3)
                keep_means(2 * k + 1, 1)
                relu1(2 * k - 2)
            keep_means(FULL - 1, 0)
            relu1(FULL - 4)
            keep_means(FULL, 1, tail=True)
            relu1(FULL - 3)
            relu1(FULL - 2)
            relu1(FULL - 1)
            relu1(FULL, tail=True)

            for layer in range(3):
                act.wait_ge(fold_dve, VAR_READY[layer])
                nc.scalar.activation(v(STD), v(VARC), ACT.Sqrt, bias=v(EPSC)).then_inc(fold_act, 1)
                if layer == 2:
                    break
                act.wait_ge(fold_dve, BIAS_READY[layer])
                bias = v(BIAS2 if layer == 0 else BIAS3)

                def relu(c, b, n=2, tail=False):
                    if tail:
                        s, d = ps[:, 2, 0:TCOLS], zc(0, True)
                    elif n == 1:
                        s, d = ps[:, 0, :], zc(c)
                    else:
                        s, d = ps[:, 2 * b:2 * b + 2, :], zc(c, n=2).rearrange("p (b n) -> p b n", b=2)
                    act.wait_ge(a_ready[layer], c + n)
                    nc.scalar.activation(d, s, ACT.Relu, bias=bias).then_inc(z_ready[layer], n)

                with act.Fori(0, PAIRS // 2) as k:
                    relu(4 * k, 0)
                    relu(4 * k + 2, 1)
                relu(FULL - 1, 0, n=1)
                relu(FULL, 1, n=1, tail=True)

            act.wait_ge(fold_dve, SHIFT_READY[2])

            def affine(c, b, free, tail=False):
                w = TCOLS if tail else COLS
                if free:
                    act.wait_ge(zT_ready, c - 1)
                nc.scalar.activation(wk(3 + b)[:, 0:w], zc(c, tail), ACT.Identity, bias=v(SHIFT3),
                                     scale=v(SCALE3)).then_inc(affine_ready, 1)

            affine(0, 0, False)
            affine(1, 1, False)
            with act.Fori(1, PAIRS) as k:
                affine(2 * k, 0, True)
                affine(2 * k + 1, 1, True)
            affine(FULL - 1, 0, True)
            affine(FULL, 1, True, tail=True)

        @block.tensor
        def _(pe):
            pe.wait_ge(fconst, 13)

            def sums(s, g, b, h, free, between, between_at, tail=False):
                n = EP if tail else P
                w = n * H
                if free:
                    pe.wait_ge(sums_copied, 2 * (s - 1))
                pe.wait_ge(mid_ready, s + 1)
                last = H * (h + 1) - 1
                lo = ps[0:LOW, 2 + h, :]
                for j, first_col in tiles_of(h):
                    q = slice(first_col * n, w)
                    pe.wait_ge(sel_ready, SELS * g + H * h + j + 1)
                    nc.tensor.matmul(ps[:, h, q], high_mid[b][0:n, j, :], sel[h][0:n, j, q],
                                     start=(j == 0), stop=(j == last))
                    if j == between_at:
                        between()
                pe.wait_ge(low_ready, s + 1)
                for j, first_col in tiles_of(h):
                    q = slice(first_col * n, w)
                    nc.tensor.matmul(lo[:, q], low_one[b][0:n, j, :], sel[h][0:n, j, q], start=(j == 0), stop=False)
                pe.wait_ge(upto_ready, s + 1)
                nc.tensor.matmul(lo[:, 0:w], pick[0:n, :], sel_upto[h][0:n, :, 0:n],
                                 start=False, stop=True).then_inc(summed, 1)

            def products(s, h, free, tail=False):
                n = EP if tail else P
                pe.wait_ge(sums_copied, 2 * (s + 1))
                if free:
                    pe.wait_ge(rows_ready, s - 1)
                for i in range(H):
                    q = slice(i * n, (i + 1) * n)
                    o = ps[0:n, 4 + h, i * LOW:(i + 1) * LOW]
                    nc.tensor.matmul(o, sums_hm[:, q], W1b_hm, start=True, stop=False)
                    ins = nc.tensor.matmul(o, sums_lo[0:LOW, q], W1b_lo[0:LOW, :], start=False, stop=True)
                ins.then_inc(y_ready, 1)

            def turn(c, b, free, tail=False):
                n, q = (TP, TG) if tail else (P, NG)
                pe.wait_ge(h_ready, c + 1)
                if free:
                    pe.wait_ge(hT_kept, c - 1)
                for j in range(q // 2):
                    ins = nc.tensor.transpose(ps[:, 6 + b, j * n:(j + 1) * n], h_tile[b][0:n, j * P:(j + 1) * P],
                                              ident[0:n, 0:n])
                ins.then_inc(hT_ready, 1)

            for c in range(2):
                turn(c, c % 2, False)
            with pe.Fori(1, AHEAD // 4) as k:
                for i in range(4):
                    turn(4 * k + i - 2, i % 2, True)
            pe.wait_ge(weights_in, 16 * len(weight_loads))
            nc.tensor.matmul(ps[:, 5, 500:501], W1c2[0:D, :], g0[0:D, :], start=True, stop=True).then_inc(shared_ready, 1)

            def step(k, i, x_before=True, first=False, tail=False, kept_tail=False):
                s, g, h, b = 4 * k + i, 2 * k + i // 2, i % 2, i // 2
                if x_before:
                    turn(s + AHEAD - 2, h, True, kept_tail)
                sums(s, g, b, h, not (first and i < 2),
                     lambda: products(s - 1, 1 - h, not (first and i < 3), tail and h == 1),
                     None if first and i == 0 else PRODUCTS_AT, tail)

            for i in range(4):
                step(0, i, first=True)
            with pe.Fori(1, XEND) as k:
                for i in range(4):
                    step(k, i)
            for i in range(4):
                step(XEND, i, kept_tail=(i == 3))
            with pe.Fori(XEND + 1, LOOPS) as k:
                for i in range(4):
                    step(k, i, x_before=False)
            for i in range(2):
                step(LOOPS, i, x_before=False, tail=True)
            products(STEPS - 1, 1, True, tail=True)

            pe.wait_ge(hT_kept, NC)
            pe.wait_ge(rows_ready, STEPS)

            def product1(c, r, free, tail=False):
                w = TCOLS if tail else COLS
                if free:
                    pe.wait_ge(added, c - 3)
                nc.tensor.matmul(ps[:, BANKS[r], 0:w], Wa[:, :], zc(c, tail), start=True, stop=True).then_inc(a1_ready, 1)

            def turn_means(c, r, b, free, tail=False):
                n, q = (TP, TG) if tail else (P, NG)
                pe.wait_ge(means_ready, c + 1)
                if free:
                    pe.wait_ge(meansT_kept, c - 1)
                for j in range(q // 2):
                    ins = nc.tensor.transpose(ps[:, 3 + b, j * n:(j + 1) * n], wk(r)[0:n, j * P:(j + 1) * P],
                                              ident[0:n, 0:n])
                ins.then_inc(meansT_ready, 1)

            for c in range(4):
                if c > 0:
                    turn_means(c - 1, c - 1, (c - 1) % 2, c > 2)
                product1(c, c, False)
            for a, z in ((1, IN_Z // 4), (IN_Z // 4, FULL // 4)):
                if a > 1:
                    pe.wait_ge(parked_in, 16 * (LATE + 1))
                with pe.Fori(a, z) as k:
                    for i in range(4):
                        turn_means(4 * k + i - 1, (i - 1) % 4, (i - 1) % 2, True)
                        product1(4 * k + i, i, True)
            turn_means(FULL - 2, 3, 1, True)
            product1(FULL - 1, 0, True)
            turn_means(FULL - 1, 0, 0, True)
            product1(FULL, 1, True, tail=True)
            turn_means(FULL, 1, 1, True, tail=True)

            def fold(layer):
                pe.wait_ge(fold_dve, MEAN_READY[layer])
                nc.tensor.matmul(ps[:, 5, 0:1], wk(4)[:, 0:P], v(MEAN), start=True, stop=True).then_inc(fold_pe, 1)
                pe.wait_ge(fold_dve, Q_READY[layer])
                nc.tensor.matmul(ps[:, 5, 1:2], wk(4)[:, 0:P], v(Q), start=True, stop=True).then_inc(fold_pe, 1)
                if layer == 2:
                    return
                pe.wait_ge(fold_dve, SHIFT_READY[layer])
                W = Wb if layer == 0 else Wa
                if layer == 1:
                    pe.wait_ge(W3_in, 32)
                nc.tensor.matmul(ps[:, 5, 2:3], W[:, :], v(SHIFT), start=True, stop=True).then_inc(fold_pe, 1)

            fold(0)
            for layer in (1, 2):
                W = Wb if layer == 1 else Wa
                pe.wait_ge(fold_dve, WEIGHTS_READY[layer - 1])
                ready, done = a_ready[layer - 1], z_ready[layer - 1]

                def product(c, bank, wait, tail=False):
                    w = TCOLS if tail else COLS
                    if wait is not None:
                        pe.wait_ge(done, wait)
                    nc.tensor.matmul(ps[:, bank, 0:w], W[:, :], zc(c, tail), start=True, stop=True).then_inc(ready, 1)

                for c in range(4):
                    product(c, c, None)
                with pe.Fori(1, PAIRS // 2) as k:
                    for i in range(4):
                        product(4 * k + i, i, 4 * k - 2 + i if i % 2 == 0 else None)
                product(FULL - 1, 0, FULL - 3)
                product(FULL, 2, FULL - 1, tail=True)
                fold(layer)

            def turn_back(c, b, free, tail=False):
                n, q = (TP, TG) if tail else (P, NG)
                pe.wait_ge(affine_ready, c + 1)
                if free:
                    pe.wait_ge(out_ready, c - 1)
                for j in range(q // 2):
                    ins = nc.tensor.transpose(ps[0:n, b, j * P:(j + 1) * P], wk(3 + b)[:, j * n:(j + 1) * n],
                                              ident[:, :])
                ins.then_inc(zT_ready, 1)

            turn_back(0, 0, False)
            turn_back(1, 1, False)
            with pe.Fori(1, PAIRS) as k:
                turn_back(2 * k, 0, True)
                turn_back(2 * k + 1, 1, True)
            turn_back(FULL - 1, 0, True)
            turn_back(FULL, 1, True, tail=True)


_INS = ["x", "src", "edge_attr_64", "L0_gnn_global_attr", "L0_gnn_W1", "L0_gnn_b1", "L0_gnn_W2", "L0_gnn_b2", "L0_gnn_W3",
        "L0_gnn_b3", "L0_gnn_g1", "L0_gnn_bt1", "L0_gnn_g2", "L0_gnn_bt2", "L0_gnn_g3", "L0_gnn_bt3"]


def kernel(**inputs):
    import numpy as _np
    import concourse.bacc as _bacc
    from concourse import mybir as _mybir
    from concourse.bass_utils import run_bass_kernel_spmd as _run

    nc = _bacc.Bacc("TRN2", target_bir_lowering=False, num_devices=1)
    arrays, args = {}, []
    for name in _INS:
        a = _np.ascontiguousarray(inputs[name])
        arrays[f"in_{name}_dram"] = a
        args.append(nc.dram_tensor(f"in_{name}_dram", a.shape, _mybir.dt.from_np(a.dtype), kind="ExternalInput").ap())
    shape = inputs["x"].shape
    out = nc.dram_tensor("out_0_dram", shape, _mybir.dt.float32, kind="ExternalOutput").ap()
    build_kernel(nc, *args, out)
    r = _run(nc, [arrays], core_ids=[0])
    return r.results[0]["out_0_dram"]
```
